# Optimizing a Trainium2 kernel written in Bass

```python
import numpy as np
import jax
import jax.numpy as jnp

def _softmax(x, axis=-1):
    return jax.nn.softmax(x, axis=axis)

def _gelu(x):
    return jax.nn.gelu(x, approximate=True)

def _silu(x):
    return jax.nn.silu(x)

def _sigmoid(x):
    return jax.nn.sigmoid(x)

def _layernorm(x, axis=-1, eps=1e-05):
    m = jnp.mean(x, axis=axis, keepdims=True)
    v = jnp.var(x, axis=axis, keepdims=True)
    return (x - m) / jnp.sqrt(v + eps)

def _scatter_add(tgt, idx, src, axis=0):
    return tgt.at[idx].add(src)

def _segment_sum(src, seg, n):
    return jax.ops.segment_sum(src, seg, n)
kernel_name = 'mk_early_fusion_d1_tok_img1024_r4_2035fe'

def setup_inputs(seed: int=0):
    np.random.seed(seed)
    _w = jnp.asarray

    def _rec_inputs():
        import jax
        import jax.numpy as jnp
        _rk = jax.random.key(seed)
        x = jax.random.uniform(jax.random.fold_in(_rk, 1), (8, 3, 256, 256), jnp.float32, 0.0, 1)
        txt = 2.40575 + 1.24603 * jax.random.normal(jax.random.fold_in(_rk, 2), (8, 77, 256), jnp.float32)
        return (x, txt)
    x, txt = _rec_inputs()

    def _L0_tok_setup():
        import jax, jax.numpy as jnp
        import numpy as np
        _GRAY_W = (0.2989, 0.587, 0.114)
        key = jax.random.key(seed)
        x = jax.random.uniform(key, (32, 3, 256, 256), dtype=jnp.float32)
        sx = jnp.array([[-3.0, 0.0, 3.0], [-10.0, 0.0, 10.0], [-3.0, 0.0, 3.0]], dtype=jnp.float32)
        scharr = jnp.stack([sx, sx.T])[:, None, :, :]
        return {'x': x, 'scharr': scharr}
    _L0_tok_all = _L0_tok_setup()
    _L0_tok_in = {k: v for k, v in _L0_tok_all.items() if k in ('scharr',)}
    del _L0_tok_all

    def _L0_attn_setup():
        import jax, jax.numpy as jnp
        import numpy as np
        B, S, DIM, SDIM = (4, 1024, 256, 64)
        key = jax.random.key(seed)
        ks = jax.random.split(key, 10)

        def lin(k, din, dout):
            return jax.random.normal(k, (din, dout), jnp.float32) / np.float32(np.sqrt(din))
        return {'x': jax.random.normal(ks[0], (B, S, DIM), jnp.float32), 'ln_g': jnp.ones((DIM,), jnp.float32), 'ln_b': jnp.zeros((DIM,), jnp.float32), 'mix_w': jax.random.normal(ks[1], (DIM, 1, 3), jnp.float32) * 0.3, 'mix_b': jnp.zeros((DIM,), jnp.float32), 'Wi': lin(ks[2], DIM, DIM), 'bi': jnp.zeros((DIM,), jnp.float32), 'Wsin': lin(ks[3], DIM, SDIM), 'bsin': jnp.zeros((SDIM,), jnp.float32), 'Wd': lin(ks[4], DIM, SDIM), 'bd': jnp.zeros((SDIM,), jnp.float32), 'Wsel': lin(ks[5], DIM, SDIM), 'bsel': jnp.zeros((SDIM,), jnp.float32), 'Wso': lin(ks[6], SDIM, DIM), 'bso': jnp.zeros((DIM,), jnp.float32), 'Wg': lin(ks[7], DIM, DIM), 'bg': jnp.zeros((DIM,), jnp.float32), 'Wout': lin(ks[8], DIM, DIM), 'bout': jnp.zeros((DIM,), jnp.float32)}
    _L0_attn_all = _L0_attn_setup()
    _L0_attn_in = {k: v for k, v in _L0_attn_all.items() if k in ('ln_g', 'ln_b', 'mix_w', 'mix_b', 'Wi', 'bi', 'Wsin', 'bsin', 'Wd', 'bd', 'Wsel', 'bsel', 'Wso', 'bso', 'Wg', 'bg', 'Wout', 'bout')}
    del _L0_attn_all

    def _L0_ffn_setup():
        import jax, jax.numpy as jnp
        import numpy as np
        import math
        D_IN = 256
        FEATURES = (1024, 1024, 256)
        BATCH, SEQ = (8, 512)

        def _conn_dense(kernel_bool, x):
            w = jnp.where(kernel_bool, jnp.float32(1.0), jnp.float32(-1.0))
            return x @ w
        key = jax.random.key(seed)
        kx, kk0, kk1, kk2 = jax.random.split(key, 4)
        x = jax.random.normal(kx, (BATCH, SEQ, D_IN), dtype=jnp.float32)
        k0 = jax.random.randint(kk0, (2 * D_IN, FEATURES[0]), 0, 2).astype(jnp.bool_)
        k1 = jax.random.randint(kk1, (FEATURES[0], FEATURES[1]), 0, 2).astype(jnp.bool_)
        k2 = jax.random.randint(kk2, (FEATURES[1], FEATURES[2]), 0, 2).astype(jnp.bool_)
        s0 = jnp.asarray(1.0 / math.sqrt(2 * D_IN), dtype=jnp.float32)
        s1 = jnp.asarray(1.0 / math.sqrt(FEATURES[0]), dtype=jnp.float32)
        s2 = jnp.asarray(1.0 / math.sqrt(FEATURES[1]), dtype=jnp.float32)
        return {'x': x, 'k0': k0, 'k1': k1, 'k2': k2, 's0': s0, 's1': s1, 's2': s2}
    _L0_ffn_all = _L0_ffn_setup()
    _L0_ffn_in = {k: v for k, v in _L0_ffn_all.items() if k in ('k0', 'k1', 'k2', 's0', 's1', 's2')}
    del _L0_ffn_all
    return {'x': x, 'txt': txt, 'L0_tok_scharr': _L0_tok_in['scharr'], 'L0_attn_ln_g': _L0_attn_in['ln_g'], 'L0_attn_ln_b': _L0_attn_in['ln_b'], 'L0_attn_mix_w': _L0_attn_in['mix_w'], 'L0_attn_mix_b': _L0_attn_in['mix_b'], 'L0_attn_Wi': _L0_attn_in['Wi'], 'L0_attn_bi': _L0_attn_in['bi'], 'L0_attn_Wsin': _L0_attn_in['Wsin'], 'L0_attn_bsin': _L0_attn_in['bsin'], 'L0_attn_Wd': _L0_attn_in['Wd'], 'L0_attn_bd': _L0_attn_in['bd'], 'L0_attn_Wsel': _L0_attn_in['Wsel'], 'L0_attn_bsel': _L0_attn_in['bsel'], 'L0_attn_Wso': _L0_attn_in['Wso'], 'L0_attn_bso': _L0_attn_in['bso'], 'L0_attn_Wg': _L0_attn_in['Wg'], 'L0_attn_bg': _L0_attn_in['bg'], 'L0_attn_Wout': _L0_attn_in['Wout'], 'L0_attn_bout': _L0_attn_in['bout'], 'L0_ffn_k0': _L0_ffn_in['k0'], 'L0_ffn_k1': _L0_ffn_in['k1'], 'L0_ffn_k2': _L0_ffn_in['k2'], 'L0_ffn_s0': _L0_ffn_in['s0'], 'L0_ffn_s1': _L0_ffn_in['s1'], 'L0_ffn_s2': _L0_ffn_in['s2']}

def reference(x, txt, L0_tok_scharr, L0_attn_ln_g, L0_attn_ln_b, L0_attn_mix_w, L0_attn_mix_b, L0_attn_Wi, L0_attn_bi, L0_attn_Wsin, L0_attn_bsin, L0_attn_Wd, L0_attn_bd, L0_attn_Wsel, L0_attn_bsel, L0_attn_Wso, L0_attn_bso, L0_attn_Wg, L0_attn_bg, L0_attn_Wout, L0_attn_bout, L0_ffn_k0, L0_ffn_k1, L0_ffn_k2, L0_ffn_s0, L0_ffn_s1, L0_ffn_s2):
    import jax
    import jax.numpy as jnp

    def _L0_tok_ref(x, scharr):
        import jax, jax.numpy as jnp
        import numpy as np
        _GRAY_W = (0.2989, 0.587, 0.114)
        w = jnp.asarray(_GRAY_W, dtype=x.dtype)
        gray = jnp.einsum('bchw,c->bhw', x, w)[:, None]
        edges = jax.lax.conv_general_dilated(gray, scharr, window_strides=(1, 1), padding='SAME', dimension_numbers=('NCHW', 'OIHW', 'NCHW'))
        abs_edges = jnp.sqrt(jnp.square(edges))
        edge = abs_edges.sum(axis=1) / 2
        return edge

    def _L0_attn_ref(x, ln_g, ln_b, mix_w, mix_b, Wi, bi, Wsin, bsin, Wd, bd, Wsel, bsel, Wso, bso, Wg, bg, Wout, bout):
        import jax, jax.numpy as jnp
        import numpy as np
        B, S, DIM, SDIM = (4, 1024, 256, 64)
        eps = 1e-05
        mu = jnp.mean(x, axis=-1, keepdims=True)
        var = jnp.mean(jnp.square(x - mu), axis=-1, keepdims=True)
        h = (x - mu) * jax.lax.rsqrt(var + eps) * ln_g + ln_b
        hc = jnp.transpose(h, (0, 2, 1))
        mixed = jax.lax.conv_general_dilated(hc, mix_w, window_strides=(1,), padding=[(1, 1)], dimension_numbers=('NCH', 'OIH', 'NCH'), feature_group_count=hc.shape[1])
        mixed = jnp.transpose(mixed + mix_b[None, :, None], (0, 2, 1))
        u = jnp.tanh(mixed @ Wi + bi)
        x_state = jnp.tanh(mixed @ Wsin + bsin)
        decay = jax.nn.sigmoid(mixed @ Wd + bd)
        select = jax.nn.sigmoid(mixed @ Wsel + bsel)

        def step(state, inp):
            dt, xt = inp
            state = dt * state + (1.0 - dt) * xt
            return (state, state)
        init = jnp.zeros((x.shape[0], x_state.shape[-1]), x.dtype)
        _, states = jax.lax.scan(step, init, (jnp.swapaxes(decay, 0, 1), jnp.swapaxes(x_state, 0, 1)))
        states = jnp.swapaxes(states, 0, 1)
        y = select * states @ Wso + bso
        g = jax.nn.sigmoid(mixed @ Wg + bg)
        out = (g * y + (1.0 - g) * u) @ Wout + bout
        return x + out

    def _L0_ffn_ref(x, k0, k1, k2, s0, s1, s2):
        import jax, jax.numpy as jnp
        import numpy as np
        import math
        D_IN = 256
        FEATURES = (1024, 1024, 256)
        BATCH, SEQ = (8, 512)

        def _conn_dense(kernel_bool, x):
            w = jnp.where(kernel_bool, jnp.float32(1.0), jnp.float32(-1.0))
            return x @ w
        h = jnp.concatenate([x, -x], axis=-1)
        h = s0 * _conn_dense(k0, h)
        h = jax.nn.relu(h) * 2
        h = s1 * _conn_dense(k1, h)
        h = jax.nn.relu(h) * 2
        h = s2 * _conn_dense(k2, h)
        return h
    h = _L0_tok_ref(x, L0_tok_scharr)
    h = jnp.concatenate([h, txt], axis=1)
    h = h + _L0_attn_ref(_layernorm(h, axis=-1), L0_attn_ln_g, L0_attn_ln_b, L0_attn_mix_w, L0_attn_mix_b, L0_attn_Wi, L0_attn_bi, L0_attn_Wsin, L0_attn_bsin, L0_attn_Wd, L0_attn_bd, L0_attn_Wsel, L0_attn_bsel, L0_attn_Wso, L0_attn_bso, L0_attn_Wg, L0_attn_bg, L0_attn_Wout, L0_attn_bout)
    h = h + _L0_ffn_ref(_layernorm(h, axis=-1), L0_ffn_k0, L0_ffn_k1, L0_ffn_k2, L0_ffn_s0, L0_ffn_s1, L0_ffn_s2)
    return h

_drawn_inputs = setup_inputs


def setup_inputs(seed=0):
    import zlib

    import numpy as np

    out = dict(_drawn_inputs(seed))
    spreads = {'L0_attn_ln_g': (1.0, 0.6),
     'L0_attn_ln_b': (0.0, 0.8),
     'L0_attn_mix_b': (0.0, 0.572),
     'L0_attn_bi': (0.0, 0.641),
     'L0_attn_bsin': (0.0, 0.8),
     'L0_attn_bd': (0.0, 0.8),
     'L0_attn_bsel': (0.0, 0.8),
     'L0_attn_bso': (0.0, 0.455),
     'L0_attn_bg': (0.0, 0.8),
     'L0_attn_bout': (0.0, 0.1)}
    factors = {'L0_attn_Wd': 7.827, 'L0_attn_Wsel': 6.424}
    for name, (base, spread) in spreads.items():
        noise = np.random.default_rng([zlib.crc32(name.encode()), seed]).standard_normal(out[name].shape)
        drawn = base * np.exp(spread * noise) if base else spread * noise
        out[name] = jnp.asarray(drawn.astype(out[name].dtype))
    for name, factor in factors.items():
        out[name] = (out[name] * factor).astype(out[name].dtype)
    return out
```

```python
from contextlib import ExitStack

import concourse.bass as bass
from concourse import mybir

ALU = mybir.AluOpType
ACT = mybir.ActivationFunctionType
F32 = mybir.dt.float32
F16 = mybir.dt.float16
U8 = mybir.dt.uint8

P = 128
GRAY = (0.2989, 0.587, 0.114)
EPS = 1e-5


class Signal:

    def __init__(self, sem, per_batch, unit=1, start=0):
        self.sem, self.per_batch, self.unit, self.start = sem, per_batch, unit, start

    def at(self, batch, k):
        return batch * (self.per_batch * self.unit) + (k * self.unit + self.start)

    def all_before(self, batch):
        return self.at(batch, 0)


def early_fusion_kernel(nc, x, txt, scharr, ln_g, ln_b, mix_w, mix_b, Wi, bi, Wsin, bsin, Wd, bd,
                        Wsel, bsel, Wso, bso, Wg, bg, Wout, bout, k0, k1, k2, s0, s1, s2, out):
    B, C, H, D = x.shape
    TXT = txt.shape[1]
    S = H + TXT
    SD = Wsin.shape[1]
    HID = k0.shape[1]
    NF = D // P
    NH = HID // P
    NT = 3
    TW = TXT + 1
    NPAIR = NH // 2
    assert H == 2 * P and D == 2 * P and SD == P // 2 and TXT < P and S <= 512 and B % 2 == 0
    H2_SCALE = 0.125

    with ExitStack() as ctx:
        def sb(name, shape, dt=F32):
            return ctx.enter_context(nc.sbuf_tensor(name, shape, dt))

        def sem(name):
            return ctx.enter_context(nc.semaphore(name))

        def sig(name, per_batch, unit=1, start=0):
            return Signal(sem(name), per_batch, unit, start)

        ident = sb("ident", [P, P])
        neg_half = sb("neg_half", [P, 2 * NT])
        taps = sb("taps", [P, 18])
        taps_in = sb("taps_in", [P, 18])
        col_g = sb("col_g", [P, NF])
        col_b = sb("col_b", [P, NF])
        col_mixw = sb("col_mixw", [P, NF, 3])
        col_mixb = sb("col_mixb", [P, NF])
        col_bi = sb("col_bi", [P, NF])
        col_bg = sb("col_bg", [P, NF])
        col_bso = sb("col_bso", [P, NF])
        col_bsin = sb("col_bsin", [SD, 1])
        col_bd = sb("col_bd", [P, 1])
        col_bsel = sb("col_bsel", [SD, 1])
        row_bout = sb("row_bout", [P, D])
        w_i = sb("w_i", [P, NF, D])
        w_g = sb("w_g", [P, NF, D])
        w_sd = sb("w_sd", [P, NF, P])
        w_sel = sb("w_sel", [P, NF, SD])
        w_so = sb("w_so", [SD, D])
        w_out = sb("w_out", [P, NF, D])
        k0_raw = sb("k0_raw", [P, 2 * NF, HID], U8)
        k1_raw = sb("k1_raw", [P, NH, HID], U8)
        k2_raw = sb("k2_raw", [P, NH, D], U8)
        w0 = sb("w0", [P, NF, HID], F16)
        w1 = sb("w1", [P, NH, HID], F16)
        w2 = sb("w2", [P, NH, D], F16)
        s_in = sb("s_in", [P, 3])
        sgn = sb("sgn", [P, 3])
        w1_aff = sb("w1_aff", [P, 2])
        s_mag = sb("s_mag", [P, 3])
        s_all = sb("s_all", [P, 2])

        img = sb("img", [P, 2, C, 2, D])
        gray_a = sb("gray_a", [P, 2, D])
        gray_b = sb("gray_b", [P, 2, D])
        gray = sb("gray", [P, 4, D + 2])
        edge = [sb(f"edge{c}", [P, 2, D]) for c in range(2)]
        edge_abs = [sb(f"edge_abs{c}", [P, 2, D]) for c in range(2)]
        h0 = sb("h0", [P, NT, D])
        st1 = sb("st1", [P, NT, 6])
        sum1 = sb("sum1", [P, NT, 2])
        dif1 = sb("dif1", [P, NT])
        sq1 = sb("sq1", [P, NT])
        mean1 = sb("mean1", [P, NT])
        dvar1 = sb("dvar1", [P, NT])
        var1 = sb("var1", [P, 2, NT])
        rs1 = sb("rs1", [P, 2, NT])
        rs1p = sb("rs1p", [P, NT])
        nmr = sb("nmr", [P, NT])
        norm = sb("norm", [P, NT, D])
        res = sb("res", [P, NT, D])
        hT = sb("hT", [P, NF, S + 2])
        mid = sb("mid", [P, NF, S])
        mixa = sb("mixa", [P, NF, S])
        mixT = sb("mixT", [P, NF, S])
        xs = sb("xs", [SD, S])
        dec = sb("dec", [SD, S])
        sel = sb("sel", [SD, S])
        nx = sb("nx", [SD, S])
        states = sb("states", [SD, S])
        selst = sb("selst", [SD, S])
        uT = sb("uT", [P, NF, S])
        gT = sb("gT", [P, NF, S])
        yu = sb("yu", [P, NF, S])
        gyu = sb("gyu", [P, NF, S])
        zT = sb("zT", [P, NF, S])
        h1 = sb("h1", [P, 2, NT, D])
        st2 = sb("st2", [P, NT, 6])
        sum2 = sb("sum2", [P, NT, 2])
        dif2 = sb("dif2", [P, NT])
        sq2 = sb("sq2", [P, NT])
        mean2 = sb("mean2", [P, NT])
        dvar2 = sb("dvar2", [P, NT])
        var2 = sb("var2", [P, NT])
        rs2 = sb("rs2", [P, NT])
        norm2 = sb("norm2", [P, NT, D])
        SW = S + 1
        x2h = sb("x2h", [P, NF, SW], F16)
        x2l = sb("x2l", [P, NF, SW], F16)
        r0h = sb("r0h", [P, NH, SW], F16)
        r0l = sb("r0l", [P, NH, SW], F16)
        r1h = sb("r1h", [P, NH, SW], F16)
        r1l = sb("r1l", [P, NH, SW], F16)
        outb = sb("outb", [P, NT, D])

        A = ctx.enter_context(nc.psum_tensor("psA", [P, 2, 512], F32))
        Bk = ctx.enter_context(nc.psum_tensor("psB", [P, 2, 512], F32))
        Q = [ctx.enter_context(nc.psum_tensor(f"psQ{i}", [P, 2, 512], F32)) for i in range(2)]

        ld_small = sem("ld_small")
        ld_mixw = sem("ld_mixw")
        ld_k = [sem(f"ld_k{i}") for i in range(3)]
        cleared = sem("cleared")
        ident_set = sem("ident_set")
        prep = sem("prep")
        w0_part = sem("w0_part")
        w_ready = [sem(f"w_ready{i}") for i in range(3)]
        ld_img = sig("ld_img", 1, 16)
        ld_txt = sig("ld_txt", 1, 16)
        shifted = sig("shifted", 4, 16)
        st_out = sig("st_out", 2, 16, start=16)
        gray_red = sig("gray_red", 1)
        edge_init = sig("edge_init", 2)
        edge_abs_ok = sig("edge_abs_ok", 2)
        hT_ok = sig("hT_ok", 2 * NF)
        mid_ok = sig("mid_ok", NF)
        gates = sig("gates", 3)
        u_ok = sig("u_ok", NF)
        g_ok = sig("g_ok", NF)
        x2h_ok = sig("x2h_ok", 1)
        r0h_ok = sig("r0h_ok", NPAIR)
        r1h_ok = sig("r1h_ok", NPAIR)
        gray_sum = sig("gray_sum", 2)
        edge_acc = sig("edge_acc", 16)
        tok_ok = sig("tok_ok", 1)
        ln1 = sig("ln1", NT + 9)
        norm_ok = sig("norm_ok", 2 * NT)
        mix = sig("mix", 2 * NF)
        state = sig("state", 3)
        yz = sig("yz", NF + 2)
        h1_ok = sig("h1_ok", NT)
        ln2 = sig("ln2", NT + 6)
        norm2_ok = sig("norm2_ok", NT)
        x2l_ok = sig("x2l_ok", 1)
        r0l_ok = sig("r0l_ok", NPAIR)
        r1l_ok = sig("r1l_ok", NPAIR)
        fin = sig("fin", 2, start=1)
        pow1 = sig("pow1", 1)
        pow2 = sig("pow2", 1)
        pe_t1 = sig("pe_t1", NF)
        pe_sd = sig("pe_sd", 2)
        pe_u = sig("pe_u", NF)
        pe_g = sig("pe_g", NF)
        pe_so = sig("pe_so", NF)
        pe_out = sig("pe_out", 2)
        pe_t2 = sig("pe_t2", 1)
        pe_f1 = sig("pe_f1", NPAIR)
        pe_f2 = sig("pe_f2", NPAIR)
        pe_f3 = sig("pe_f3", 2)

        def wait(eng, signal, batch, k):
            eng.wait_ge(signal.sem, signal.at(batch, k))

        def wait_before(eng, signal, batch):
            if not (isinstance(batch, int) and batch < 1):
                eng.wait_ge(signal.sem, signal.all_before(batch))

        N_SMALL = 15
        N_MIXW = 7
        block = ctx.enter_context(nc.Block())

        @block.sync
        def _(sp):
            def load_image(n, par):
                if not (isinstance(n, int) and n < 2):
                    wait(sp, gray_sum, n - 2, 2)
                sp.dma_start(img[:, par], x[n].rearrange("c (p j) w -> p c j w", j=2)).then_inc(ld_img.sem, 16)

            def load_text(n):
                wait_before(sp, norm_ok, n)
                sp.dma_start(h0[0:TXT, 2], txt[n]).then_inc(ld_txt.sem, 16)

            def shift_rows(n):
                wait(sp, gray_sum, n, 2)
                lo, hi = 112, P - 1
                sp.dma_start(gray[1:1 + lo, 0, 1:D + 1], gray[0:lo, 2, 1:D + 1]).then_inc(shifted.sem, 16)
                sp.dma_start(gray[0:lo, 3, 1:D + 1], gray[1:1 + lo, 1, 1:D + 1]).then_inc(shifted.sem, 16)
                sp.dma_start(gray[1 + lo:1 + hi, 0, 1:D + 1], gray[lo:hi, 2, 1:D + 1]).then_inc(shifted.sem, 16)
                sp.dma_start(gray[lo:hi, 3, 1:D + 1], gray[1 + lo:1 + hi, 1, 1:D + 1]).then_inc(shifted.sem, 16)

            def store(n):
                wait(sp, fin, n, 1)
                sp.dma_start(out[n, 0:H].rearrange("(p j) w -> p j w", j=2), outb[:, 0:2]).then_inc(st_out.sem, 16)
                wait(sp, fin, n, 2)
                sp.dma_start(out[n, H:S], outb[0:TXT, 2]).then_inc(st_out.sem, 16)

            sp.sem_inc(st_out.sem, st_out.start)
            load_image(0, 0)
            sp.dma_start(taps_in[:], scharr.rearrange("a b c d -> (a b c d)").partition_broadcast(P)).then_inc(ld_small, 16)
            sp.dma_start(row_bout[:], bout.partition_broadcast(P)).then_inc(ld_small, 16)
            for i, s in enumerate((s0, s1, s2)):
                sp.dma_start(s_in[:, i:i + 1], s.partition_broadcast(P)).then_inc(ld_small, 16)
            sp.wait_ge(cleared, 2)
            load_text(0)
            for dst, src in ((col_g, ln_g), (col_b, ln_b), (col_mixb, mix_b), (col_bi, bi), (col_bg, bg), (col_bso, bso)):
                sp.dma_start(dst[:], src.rearrange("(f p) -> p f", p=P), allow_slow_non_contiguous=True).then_inc(ld_small, 16)
            sp.dma_start(col_mixw[:], mix_w.rearrange("(f p) a t -> p f (a t)", p=P)).then_inc(ld_small, 16)
            for dst, src in ((col_bsin[:], bsin), (col_bd[SD:P], bd), (col_bsel[:], bsel)):
                sp.dma_start(dst, src.rearrange("(p a) -> p a", a=1)).then_inc(ld_small, 16)
            sp.dma_start(w_sd[:, :, 0:SD], Wsin.rearrange("(f p) n -> p f n", p=P)).then_inc(ld_mixw, 16)
            sp.dma_start(w_sd[:, :, SD:P], Wd.rearrange("(f p) n -> p f n", p=P)).then_inc(ld_mixw, 16)
            sp.dma_start(w_sel[:], Wsel.rearrange("(f p) n -> p f n", p=P)).then_inc(ld_mixw, 16)
            sp.dma_start(w_i[:], Wi.rearrange("(f p) n -> p f n", p=P)).then_inc(ld_mixw, 16)
            sp.dma_start(w_g[:], Wg.rearrange("(f p) n -> p f n", p=P)).then_inc(ld_mixw, 16)
            shift_rows(0)
            load_image(1, 1)
            sp.dma_start(w_so[:], Wso).then_inc(ld_mixw, 16)
            sp.dma_start(w_out[:], Wout.rearrange("(f p) n -> p f n", p=P)).then_inc(ld_mixw, 16)
            sp.dma_start(k0_raw[:], k0.rearrange("(f p) n -> p f n", p=P)).then_inc(ld_k[0], 16)
            sp.dma_start(k1_raw[:], k1.rearrange("(f p) n -> p f n", p=P)).then_inc(ld_k[1], 16)
            sp.dma_start(k2_raw[:], k2.rearrange("(f p) n -> p f n", p=P)).then_inc(ld_k[2], 16)
            load_text(1)
            shift_rows(1)
            with sp.Fori(0, B - 3, 2) as b0:
                for par in range(2):
                    b = b0 + par
                    load_image(b + 2, par)
                    load_text(b + 2)
                    shift_rows(b + 2)
                    store(b)
            store(B - 2)
            store(B - 1)
            sp.wait_ge(st_out.sem, st_out.at(B - 1, 2))

        @block.gpsimd
        def _(pool):
            nc.gpsimd.memset(gray[:], 0.0).then_inc(cleared, 1)
            nc.gpsimd.memset(h0[:, 2], 0.0).then_inc(cleared, 1)
            nc.gpsimd.memset(neg_half[:], -0.5).then_inc(cleared, 1)
            nc.gpsimd.memset(hT[:], 0.0).then_inc(cleared, 1)
            nc.gpsimd.memset(h1[:, :, 2], 0.0).then_inc(cleared, 1)
            nc.gpsimd.memset(ident[:], 0.0).then_inc(ident_set, 1)
            pool.wait_ge(ident_set, 1)
            nc.gpsimd.affine_select(out=ident[:], in_=ident[:], compare_op=ALU.not_equal, fill=1.0, base=0,
                                    pattern=[[-1, P]], channel_multiplier=1).then_inc(ident_set, 1)
            pool.wait_ge(cleared, 5)

            def rsqrt1(n):
                wait(pool, ln1, n, NT + 7)
                nc.gpsimd.tensor_tensor(rs1[:].rearrange("p a t -> p (a t)"), var1[:].rearrange("p a t -> p (a t)"),
                                        neg_half[:], ALU.pow).then_inc(pow1.sem, 1)

            def rsqrt2(n):
                wait(pool, ln2, n, NT + 6)
                nc.gpsimd.tensor_tensor(rs2[:], var2[:], neg_half[:, 0:NT], ALU.pow).then_inc(pow2.sem, 1)

            rsqrt1(0)
            rsqrt2(0)
            rsqrt1(1)
            with pool.Fori(0, B - 3, 2) as b0:
                for par in range(2):
                    rsqrt2(b0 + par + 1)
                    rsqrt1(b0 + par + 2)
            rsqrt2(B - 1)

        @block.scalar
        def _(act):
            act_fn = nc.scalar.activation

            def gray_first(n, par):
                wait(act, ld_img, n, 1)
                act_fn(gray_a[:], img[:, par, 0], ACT.Copy, scale=GRAY[0]).then_inc(gray_red.sem, 1)

            def edge_first(n):
                wait(act, gray_sum, n, 2)
                for c in range(2):
                    act_fn(edge[c][:], gray[:, 1:3, 0:D], ACT.Copy, scale=taps[:, 9 * c + 3:9 * c + 4]).then_inc(edge_init.sem, 1)

            def edge_fold(n):
                for c in range(2):
                    wait(act, edge_acc, n, 15 + c)
                    act_fn(edge_abs[c][:], edge[c][:], ACT.Abs).then_inc(edge_abs_ok.sem, 1)

            def to_feature_major(n):
                for f in range(NF):
                    wait(act, pe_t1, n, f + 1)
                    act_fn(hT[:, f, 1:1 + H].rearrange("q (p j) -> q j p", j=2),
                           A[:, f, 0:H].rearrange("q (j p) -> q j p", j=2), ACT.Identity,
                           scale=col_g[:, f:f + 1], bias=col_b[:, f:f + 1]).then_inc(hT_ok.sem, 1)
                    act_fn(hT[:, f, 1 + H:1 + S], A[:, f, H:S], ACT.Identity,
                           scale=col_g[:, f:f + 1], bias=col_b[:, f:f + 1]).then_inc(hT_ok.sem, 1)
                for f in range(NF):
                    wait(act, hT_ok, n, 2 * f + 2)
                    act_fn(mid[:, f], hT[:, f, 1:1 + S], ACT.Identity,
                           scale=col_mixw[:, f, 1:2], bias=col_mixb[:, f:f + 1]).then_inc(mid_ok.sem, 1)

            def gate_state(n):
                wait(act, pe_sd, n, 1)
                act_fn(dec[:], Bk[SD:P, 0, 0:S], ACT.Sigmoid, bias=col_bd[SD:P]).then_inc(gates.sem, 1)
                act_fn(xs[:], Bk[0:SD, 0, 0:S], ACT.Tanh, bias=col_bsin[:]).then_inc(gates.sem, 1)
                wait(act, pe_sd, n, 2)
                act_fn(sel[:], Bk[0:SD, 1, 0:S], ACT.Sigmoid, bias=col_bsel[:]).then_inc(gates.sem, 1)

            def gate_u(n):
                for f in range(NF):
                    wait(act, pe_u, n, f + 1)
                    act_fn(uT[:, f], A[:, f, 0:S], ACT.Tanh, bias=col_bi[:, f:f + 1]).then_inc(u_ok.sem, 1)

            def gate_g(n):
                for f in range(NF):
                    wait(act, pe_g, n, f + 1)
                    act_fn(gT[:, f], Bk[:, f, 0:S], ACT.Sigmoid, bias=col_bg[:, f:f + 1]).then_inc(g_ok.sem, 1)

            def x2_high(n):
                wait(act, pe_t2, n, 1)
                act_fn(x2h[:, :, 0:S], A[:, :, 0:S], ACT.Copy).then_inc(x2h_ok.sem, 1)

            def hidden_high(n, par, q, produced, dst, done):
                wait(act, produced, n, q + 1)
                act_fn(dst[:, 2 * q:2 * q + 2, 0:S], Q[(q + par) % 2][:, :, 0:S], ACT.Relu).then_inc(done.sem, 1)

            def h0_high(n, par, q):
                hidden_high(n, par, q, pe_f1, r0h, r0h_ok)

            def h1_high(n, par, q):
                hidden_high(n, par, q, pe_f2, r1h, r1h_ok)

            def step(b, par, mixer=True, tokens=True):
                n, t = b + 1, b + 2
                for q in range(NPAIR):
                    h0_high(b, par, q)
                if mixer:
                    to_feature_major(n)
                if tokens:
                    gray_first(t, par)
                    edge_first(t)
                h1_high(b, par, 0)
                if mixer:
                    gate_state(n)
                    gate_u(n)
                    gate_g(n)
                h1_high(b, par, 1)
                h1_high(b, par, 2)
                if tokens:
                    edge_fold(t)
                h1_high(b, par, 3)
                if mixer:
                    x2_high(n)

            gray_first(0, 0)
            act.wait_ge(prep, 1)
            edge_first(0)
            edge_fold(0)
            act.wait_ge(ld_small, 16 * N_SMALL)
            act.wait_ge(cleared, 5)
            to_feature_major(0)
            gray_first(1, 1)
            edge_first(1)
            gate_state(0)
            gate_u(0)
            gate_g(0)
            edge_fold(1)
            act.wait_ge(prep, 5)
            act.wait_ge(ld_k[1], 16)
            act_fn(w1[:], k1_raw[:], ACT.Identity, scale=w1_aff[:, 0:1], bias=w1_aff[:, 1:2]).then_inc(w_ready[1], 1)
            x2_high(0)
            with act.Fori(0, B - 3, 2) as b0:
                for par in range(2):
                    step(b0 + par, par)
            step(B - 2, 0, tokens=False)
            step(B - 1, 1, mixer=False, tokens=False)

        @block.vector
        def _(dve):
            V = nc.vector

            def gray_rest(n, par):
                wait(dve, gray_red, n, 1)
                V.scalar_tensor_tensor(gray_b[:], img[:, par, 1], GRAY[1], gray_a[:], ALU.mult, ALU.add).then_inc(gray_sum.sem, 1)
                wait(dve, gray_sum, n, 1)
                V.scalar_tensor_tensor(gray[:, 1:3, 1:D + 1], img[:, par, 2], GRAY[2], gray_b[:], ALU.mult, ALU.add).then_inc(gray_sum.sem, 1)

            order = [(1, 1), (1, 2), (0, 0), (0, 1), (0, 2), (2, 0), (2, 1), (2, 2)]

            def edges(n, first, last):
                for k in range(first, last):
                    c, (dy, dx) = k % 2, order[k // 2]
                    if k < 2:
                        wait(dve, edge_init, n, k + 1)
                    else:
                        wait(dve, edge_acc, n, k - 1)
                    if k == 4:
                        wait(dve, shifted, n, 4)
                    tap = 9 * c + 3 * dy + dx
                    V.scalar_tensor_tensor(edge[c][:], gray[:, dy:dy + 2, dx:dx + D], taps[:, tap:tap + 1], edge[c][:],
                                           ALU.mult, ALU.add).then_inc(edge_acc.sem, 1)

            def tokens_done(n):
                wait(dve, edge_abs_ok, n, 2)
                V.tensor_tensor(h0[:, 0:2], edge_abs[0][:], edge_abs[1][:], ALU.add).then_inc(tok_ok.sem, 1)

            def moments(n, done, st, total, dif, sq, mean, dvar):
                wait(dve, done, n, NT)
                V.tensor_tensor(total[:], st[:, :, 1:3], st[:, :, 4:6], ALU.add).then_inc(done.sem, 1)
                V.tensor_tensor(dif[:], st[:, :, 1], st[:, :, 4], ALU.subtract).then_inc(done.sem, 1)
                wait(dve, done, n, NT + 2)
                V.tensor_tensor(sq[:], dif[:], dif[:], ALU.mult).then_inc(done.sem, 1)
                V.tensor_scalar(mean[:], total[:, :, 0], 0.5, None, ALU.mult).then_inc(done.sem, 1)
                wait(dve, done, n, NT + 3)
                V.scalar_tensor_tensor(dvar[:], sq[:], D / 4, total[:, :, 1], ALU.mult, ALU.add).then_inc(done.sem, 1)
                wait(dve, done, n, NT + 5)

            def norm1_stats(n):
                wait(dve, ld_txt, n, 1)
                wait(dve, tok_ok, n, 1)
                for t in range(NT):
                    V.bn_stats(st1[:, t], h0[:, t]).then_inc(ln1.sem, 1)
                moments(n, ln1, st1, sum1, dif1, sq1, mean1, dvar1)
                V.tensor_scalar(var1[:, 0], dvar1[:], 1.0 / D, EPS, ALU.mult, ALU.add).then_inc(ln1.sem, 1)
                V.tensor_scalar(var1[:, 1], dvar1[:], (1.0 + EPS) / D, EPS * EPS, ALU.mult, ALU.add).then_inc(ln1.sem, 1)

            def norm1_apply(n):
                wait(dve, pow1, n, 1)
                V.tensor_scalar(rs1p[:], rs1[:, 0], 1.0, None, ALU.add).then_inc(ln1.sem, 1)
                for t in range(NT):
                    V.tensor_scalar(norm[:, t], h0[:, t], mean1[:, t:t + 1], rs1[:, 1, t:t + 1],
                                    ALU.subtract, ALU.mult).then_inc(norm_ok.sem, 1)
                wait(dve, ln1, n, NT + 8)
                V.scalar_tensor_tensor(nmr[:], mean1[:], -1.0, rs1[:, 0], ALU.mult, ALU.mult).then_inc(ln1.sem, 1)
                for t in range(NT):
                    V.scalar_tensor_tensor(res[:, t], h0[:, t], rs1p[:, t:t + 1], row_bout[:],
                                           ALU.mult, ALU.add).then_inc(norm_ok.sem, 1)

            def mix_tokens(n):
                for f in range(NF):
                    wait(dve, mid_ok, n, f + 1)
                    V.scalar_tensor_tensor(mixa[:, f], hT[:, f, 0:S], col_mixw[:, f, 0:1], mid[:, f],
                                           ALU.mult, ALU.add).then_inc(mix.sem, 1)
                for f in range(NF):
                    wait(dve, mix, n, f + 1)
                    V.scalar_tensor_tensor(mixT[:, f], hT[:, f, 2:S + 2], col_mixw[:, f, 2:3], mixa[:, f],
                                           ALU.mult, ALU.add).then_inc(mix.sem, 1)

            def scan_states(n):
                wait(dve, gates, n, 2)
                V.scalar_tensor_tensor(nx[:], dec[:], 1.0, xs[:], ALU.subtract, ALU.mult).then_inc(state.sem, 1)
                wait(dve, state, n, 1)
                V.tensor_tensor_scan(states[:], dec[:], nx[:], 0.0, ALU.mult, ALU.subtract).then_inc(state.sem, 1)
                wait(dve, gates, n, 3)
                wait(dve, state, n, 2)
                V.tensor_tensor(selst[:], states[:], sel[:], ALU.mult).then_inc(state.sem, 1)

            def blend(n):
                for f in range(NF):
                    wait(dve, pe_so, n, f + 1)
                    wait(dve, u_ok, n, f + 1)
                    V.scalar_tensor_tensor(yu[:, f], A[:, f, 0:S], col_bso[:, f:f + 1], uT[:, f],
                                           ALU.add, ALU.subtract).then_inc(yz.sem, 1)
                wait(dve, yz, n, NF)
                wait(dve, g_ok, n, NF)
                V.tensor_tensor(gyu[:], gT[:], yu[:], ALU.mult).then_inc(yz.sem, 1)
                wait(dve, yz, n, NF + 1)
                V.tensor_tensor(zT[:], gyu[:], uT[:], ALU.add).then_inc(yz.sem, 1)

            def residual(n, par):
                wait(dve, ln1, n, NT + 9)
                wait(dve, norm_ok, n, 2 * NT)
                for t in range(NT):
                    if t != 1:
                        wait(dve, pe_out, n, t // 2 + 1)
                    rows = P if t < 2 else TXT
                    src = Bk[0:rows, t // 2, (t % 2) * D:(t % 2 + 1) * D]
                    V.scalar_tensor_tensor(h1[0:rows, par, t], src, nmr[0:rows, t:t + 1], res[0:rows, t],
                                           ALU.add, ALU.add).then_inc(h1_ok.sem, 1)

            def norm2_stats(n, par):
                for t in range(NT):
                    wait(dve, h1_ok, n, t + 1)
                    V.bn_stats(st2[:, t], h1[:, par, t]).then_inc(ln2.sem, 1)
                moments(n, ln2, st2, sum2, dif2, sq2, mean2, dvar2)
                V.tensor_scalar(var2[:], dvar2[:], 1.0 / D, EPS, ALU.mult, ALU.add).then_inc(ln2.sem, 1)

            def norm2_apply(n, par):
                wait(dve, pow2, n, 1)
                for t in range(NT):
                    V.tensor_scalar(norm2[:, t], h1[:, par, t], mean2[:, t:t + 1], rs2[:, t:t + 1],
                                    ALU.subtract, ALU.mult).then_inc(norm2_ok.sem, 1)

            def x2_low(n):
                wait(dve, x2h_ok, n, 1)
                V.tensor_tensor(x2l[:, :, 0:S], A[:, :, 0:S], x2h[:, :, 0:S], ALU.subtract).then_inc(x2l_ok.sem, 1)

            def hidden_low(n, par, q, high_ok, high, dst, done):
                wait(dve, high_ok, n, q + 1)
                V.scalar_tensor_tensor(dst[:, 2 * q:2 * q + 2, 0:S], Q[(q + par) % 2][:, :, 0:S], 0.0,
                                       high[:, 2 * q:2 * q + 2, 0:S], ALU.max, ALU.subtract).then_inc(done.sem, 1)

            def h0_low(n, par, q):
                hidden_low(n, par, q, r0h_ok, r0h, r0l, r0l_ok)

            def h1_low(n, par, q):
                hidden_low(n, par, q, r1h_ok, r1h, r1l, r1l_ok)

            def finish(n, par):
                wait_before(dve, st_out, n)
                wait(dve, pe_f3, n, 1)
                V.scalar_tensor_tensor(outb[:, 0:2].rearrange("p t w -> p (t w)"), Q[par][:, 0, 0:2 * D],
                                       s_all[:, 1:2], h1[:, par, 0:2].rearrange("p t w -> p (t w)"),
                                       ALU.mult, ALU.add).then_inc(fin.sem, 1)
                wait(dve, pe_f3, n, 2)
                V.scalar_tensor_tensor(outb[0:TXT, 2], Q[par][0:TXT, 1, 0:D], s_all[0:TXT, 1:2],
                                       h1[0:TXT, par, 2], ALU.mult, ALU.add).then_inc(fin.sem, 1)

            def step(b, par, mixer=True, tokens=True):
                n, t, other = b + 1, b + 2, 1 - par
                for q in range(NPAIR):
                    h0_low(b, par, q)
                if mixer:
                    mix_tokens(n)
                if tokens:
                    gray_rest(t, par)
                    edges(t, 0, 2)
                h1_low(b, par, 0)
                if mixer:
                    scan_states(n)
                if tokens:
                    edges(t, 2, 10)
                h1_low(b, par, 1)
                if mixer:
                    blend(n)
                if tokens:
                    edges(t, 10, 16)
                h1_low(b, par, 2)
                if tokens:
                    tokens_done(t)
                if mixer:
                    residual(n, other)
                    norm2_stats(n, other)
                    norm2_apply(n, other)
                h1_low(b, par, 3)
                if tokens:
                    norm1_stats(t)
                if mixer:
                    x2_low(n)
                if tokens:
                    norm1_apply(t)
                finish(b, par)

            dve.sem_inc(fin.sem, fin.start)
            dve.wait_ge(cleared, 5)
            dve.wait_ge(ld_small, 16 * N_SMALL)
            V.tensor_scalar(taps[:], taps_in[:], 0.5, None, ALU.mult).then_inc(prep, 1)
            V.tensor_scalar(sgn[:], s_in[:], 0.0, None, ALU.is_ge).then_inc(prep, 1)
            dve.wait_ge(prep, 2)
            V.tensor_scalar(sgn[:], sgn[:], 2.0, -1.0, ALU.mult, ALU.add).then_inc(prep, 1)
            dve.wait_ge(prep, 3)
            V.tensor_scalar(w1_aff[:, 0:1], sgn[:, 1:2], 2.0 * H2_SCALE, None, ALU.mult).then_inc(prep, 1)
            V.tensor_scalar(w1_aff[:, 1:2], sgn[:, 1:2], -H2_SCALE, None, ALU.mult).then_inc(prep, 1)
            V.tensor_tensor(s_mag[:], s_in[:], sgn[:], ALU.mult).then_inc(prep, 1)
            dve.wait_ge(prep, 6)
            V.scalar_tensor_tensor(s_all[:, 0:1], s_mag[:, 0:1], 8.0 / H2_SCALE, s_mag[:, 1:2], ALU.mult, ALU.mult).then_inc(prep, 1)
            dve.wait_ge(prep, 7)
            V.tensor_tensor(s_all[:, 1:2], s_all[:, 0:1], s_in[:, 2:3], ALU.mult).then_inc(prep, 1)
            gray_rest(0, 0)
            edges(0, 0, 16)
            tokens_done(0)
            norm1_stats(0)
            norm1_apply(0)
            mix_tokens(0)
            gray_rest(1, 1)
            edges(1, 0, 8)
            scan_states(0)
            edges(1, 8, 16)
            tokens_done(1)
            blend(0)
            dve.wait_ge(ld_k[0], 16)
            V.tensor_tensor(w0[:], k0_raw[:, 0:NF], k0_raw[:, NF:2 * NF], ALU.subtract).then_inc(w0_part, 1)
            dve.wait_ge(w0_part, 1)
            V.tensor_scalar(w0[:], w0[:], sgn[:, 0:1], None, ALU.mult).then_inc(w_ready[0], 1)
            residual(0, 0)
            norm2_stats(0, 0)
            norm2_apply(0, 0)
            dve.wait_ge(ld_k[2], 16)
            V.tensor_scalar(w2[:], k2_raw[:], 2.0, -1.0, ALU.mult, ALU.add).then_inc(w_ready[2], 1)
            norm1_stats(1)
            x2_low(0)
            norm1_apply(1)
            with dve.Fori(0, B - 3, 2) as b0:
                for par in range(2):
                    step(b0 + par, par)
            step(B - 2, 0, tokens=False)
            step(B - 1, 1, mixer=False, tokens=False)

        @block.tensor
        def _(pe):
            mm = nc.tensor.matmul

            def transposes(bank, f, src):
                for t in range(NT):
                    rows = P if t < 2 else TW
                    last = nc.tensor.transpose(bank[:, f, t * P:t * P + rows], src[0:rows, t, f * P:(f + 1) * P],
                                               ident[0:rows, 0:rows])
                return last

            def transpose_norm1(n):
                for f in range(NF):
                    if f == 0:
                        wait(pe, norm_ok, n, NT)
                    transposes(A, f, norm).then_inc(pe_t1.sem, 1)

            def project(dst, w, lo, width):
                for k in range(NF):
                    last = mm(dst, w[:, k, lo:lo + width], mixT[:, k], start=(k == 0), stop=(k == NF - 1))
                return last

            def state_inputs(n):
                wait(pe, mix, n, 2 * NF)
                wait_before(pe, h1_ok, n)
                project(Bk[:, 0, 0:S], w_sd, 0, P).then_inc(pe_sd.sem, 1)
                project(Bk[0:SD, 1, 0:S], w_sel, 0, SD).then_inc(pe_sd.sem, 1)

            def u_inputs(n):
                for f in range(NF):
                    project(A[:, f, 0:S], w_i, f * P, P).then_inc(pe_u.sem, 1)

            def g_inputs(n):
                wait(pe, gates, n, 3)
                for f in range(NF):
                    project(Bk[:, f, 0:S], w_g, f * P, P).then_inc(pe_g.sem, 1)

            def state_output(n):
                wait(pe, state, n, 3)
                wait(pe, u_ok, n, NF)
                for f in range(NF):
                    mm(A[:, f, 0:S], w_so[:, f * P:(f + 1) * P], selst[:], start=True, stop=True).then_inc(pe_so.sem, 1)

            def mixer_output(n):
                wait(pe, yz, n, NF + 2)
                for t in range(NT):
                    rows = P if t < 2 else TXT
                    for k in range(NF):
                        lhs = zT[:, k, t:H:2] if t < 2 else zT[:, k, H:S]
                        last = mm(Bk[0:rows, t // 2, (t % 2) * D:(t % 2 + 1) * D], lhs, w_out[:, k],
                                  start=(k == 0), stop=(k == NF - 1))
                    if t > 0:
                        last.then_inc(pe_out.sem, 1)

            def transpose_norm2(n):
                wait(pe, norm2_ok, n, NT)
                for f in range(NF):
                    last = transposes(A, f, norm2)
                last.then_inc(pe_t2.sem, 1)

            def both(dst, lhs, k, high, low, first, last):
                mm(dst, lhs, high[:, k, 0:S], start=first, stop=False)
                return mm(dst, lhs, low[:, k, 0:S], start=False, stop=last)

            def layer1(n, par, q):
                if q == 0:
                    wait(pe, x2l_ok, n, 1)
                elif q == 1:
                    wait_before(pe, fin, n)
                else:
                    wait(pe, r0l_ok, n, q - 1)
                for m in range(2):
                    for k in range(NF):
                        col = (2 * q + m) * P
                        last = both(Q[(q + par) % 2][:, m, 0:S], w0[:, k, col:col + P], k, x2h, x2l,
                                    k == 0, k == NF - 1)
                last.then_inc(pe_f1.sem, 1)

            def layer2(n, par, q):
                if q == 0:
                    wait(pe, r0l_ok, n, NPAIR - 1)
                if q >= 2:
                    wait(pe, r1l_ok, n, q - 1)
                for ks in (range(0, NH - 2), range(NH - 2, NH)):
                    if q == 0 and ks[0]:
                        wait(pe, r0l_ok, n, NPAIR)
                    if q == 1 and not ks[0]:
                        wait(pe, r0l_ok, n, NPAIR)
                    for m in range(2):
                        col = (2 * q + m) * P
                        for k in ks:
                            last = both(Q[(q + par) % 2][:, m, 0:S], w1[:, k, col:col + P], k, r0h, r0l,
                                        k == 0, k == NH - 1)
                last.then_inc(pe_f2.sem, 1)

            def layer3(n, par, ks):
                for t in range(NT):
                    rows = P if t < 2 else TXT
                    dst = Q[par][0:rows, t // 2, (t % 2) * D:(t % 2 + 1) * D]
                    for k in ks:
                        for part, r1 in enumerate((r1h, r1l)):
                            last = mm(dst, r1[:, k, t * P:t * P + rows], w2[:, k],
                                      start=(k == 0 and part == 0 and t != 1), stop=(k == NH - 1 and part == 1),
                                      skip_group_check=True)
                    if t > 0 and ks[-1] == NH - 1:
                        last.then_inc(pe_f3.sem, 1)

            def step(b, par, mixer=True):
                n = b + 1
                layer1(b, par, 0)
                layer1(b, par, 1)
                layer1(b, par, 2)
                if mixer:
                    transpose_norm1(n)
                layer1(b, par, 3)
                layer2(b, par, 0)
                if mixer:
                    state_inputs(n)
                    u_inputs(n)
                    g_inputs(n)
                layer2(b, par, 1)
                if mixer:
                    state_output(n)
                layer2(b, par, 2)
                if mixer:
                    mixer_output(n)
                layer2(b, par, 3)
                wait(pe, r1l_ok, b, NPAIR - 1)
                layer3(b, par, range(0, NH - 2))
                if mixer:
                    transpose_norm2(n)
                wait(pe, r1l_ok, b, NPAIR)
                layer3(b, par, range(NH - 2, NH))

            pe.wait_ge(ident_set, 2)
            transpose_norm1(0)
            pe.wait_ge(ld_mixw, 16 * N_MIXW)
            state_inputs(0)
            u_inputs(0)
            g_inputs(0)
            state_output(0)
            mixer_output(0)
            transpose_norm2(0)
            pe.wait_ge(w_ready[0], 1)
            pe.wait_ge(w_ready[1], 1)
            pe.wait_ge(w_ready[2], 1)
            with pe.Fori(0, B - 3, 2) as b0:
                for par in range(2):
                    step(b0 + par, par)
            step(B - 2, 0)
            step(B - 1, 1, mixer=False)


_INS = ['x', 'txt', 'L0_tok_scharr', 'L0_attn_ln_g', 'L0_attn_ln_b', 'L0_attn_mix_w', 'L0_attn_mix_b', 'L0_attn_Wi',
        'L0_attn_bi', 'L0_attn_Wsin', 'L0_attn_bsin', 'L0_attn_Wd', 'L0_attn_bd', 'L0_attn_Wsel', 'L0_attn_bsel',
        'L0_attn_Wso', 'L0_attn_bso', 'L0_attn_Wg', 'L0_attn_bg', 'L0_attn_Wout', 'L0_attn_bout', 'L0_ffn_k0',
        'L0_ffn_k1', 'L0_ffn_k2', 'L0_ffn_s0', 'L0_ffn_s1', 'L0_ffn_s2']


def kernel(**inputs):
    import numpy as _np
    import concourse.bacc as _bacc
    from concourse import mybir as _mybir
    from concourse.bass_utils import run_bass_kernel_spmd as _run

    nc = _bacc.Bacc("TRN2", target_bir_lowering=False, num_devices=1)
    arrays, args = {}, []
    for name in _INS:
        a = _np.ascontiguousarray(inputs[name])
        arrays[f"in_{name}_dram"] = a
        args.append(nc.dram_tensor(f"in_{name}_dram", a.shape, _mybir.dt.from_np(a.dtype), kind="ExternalInput").ap())
    shape = (inputs['x'].shape[0], inputs['x'].shape[2] + inputs['txt'].shape[1], inputs['x'].shape[3])
    args.append(nc.dram_tensor("out_0_dram", shape, _mybir.dt.float32, kind="ExternalOutput").ap())
    early_fusion_kernel(nc, *args)
    r = _run(nc, [arrays], core_ids=[0])
    return r.results[0]["out_0_dram"]
```

```python
from contextlib import ExitStack

import concourse.bass as bass
from concourse import mybir

ALU = mybir.AluOpType
ACT = mybir.ActivationFunctionType
F32 = mybir.dt.float32
F16 = mybir.dt.float16
U8 = mybir.dt.uint8

P = 128
GRAY = (0.2989, 0.587, 0.114)
EPS = 1e-5


class Signal:

    def __init__(self, sem, per_batch, unit=1, start=0):
        self.sem, self.per_batch, self.unit, self.start = sem, per_batch, unit, start

    def at(self, batch, k):
        return batch * (self.per_batch * self.unit) + (k * self.unit + self.start)

    def all_before(self, batch):
        return self.at(batch, 0)


ROW_PARTS = (("scharr", 18), ("s", 3), ("bout", 256))
COL_PARTS = (("ln_g", 2), ("ln_b", 2), ("mix_w", 6), ("mix_b", 2), ("bi", 2), ("bg", 2), ("bso", 2),
             ("bsin_bd", 1), ("bsel", 1))
W_PARTS = (("Wsin_Wd", 128), ("Wsel", 64), ("Wi", 256), ("Wg", 256))


def spans(parts):
    at, found = 0, {}
    for name, width in parts:
        found[name] = (at, at + width)
        at += width
    return found, at


def early_fusion_kernel(nc, x, txt, row_pack, col_pack, w_pack, Wso, Wout, k0, k1, k2, out):
    B, C, H, D = x.shape
    TXT = txt.shape[1]
    S = H + TXT
    SD = Wso.shape[0]
    HID = k0.shape[1]
    NF = D // P
    NH = HID // P
    NT = 3
    TW = TXT + 1
    NPAIR = NH // 2
    assert H == 2 * P and D == 2 * P and SD == P // 2 and TXT < P and S <= 512 and B % 2 == 0
    H2_SCALE = 0.125

    with ExitStack() as ctx:
        def sb(name, shape, dt=F32):
            return ctx.enter_context(nc.sbuf_tensor(name, shape, dt))

        def sem(name):
            return ctx.enter_context(nc.semaphore(name))

        def sig(name, per_batch, unit=1, start=0):
            return Signal(sem(name), per_batch, unit, start)

        identw = sb("identw", [P, P + 2])
        ident = identw[:, 1:P + 1]
        tap_diag = sb("tap_diag", [P, 3, 3, P])
        tap_up = sb("tap_up", [P, 3, P])
        tap_down = sb("tap_down", [P, 3, P])
        neg_half = sb("neg_half", [P, 2 * NT])
        row_at, row_width = spans(ROW_PARTS)
        col_at, col_width = spans(COL_PARTS)
        w_at, w_width = spans(W_PARTS)
        rows_all = sb("rows_all", [P, row_width])
        cols = sb("cols", [P, col_width])
        w_in = sb("w_in", [P, NF, w_width])

        def col(name):
            return cols[:, slice(*col_at[name])]

        taps_in = rows_all[:, slice(*row_at["scharr"])]
        s_in = rows_all[:, slice(*row_at["s"])]
        row_bout = rows_all[:, slice(*row_at["bout"])]
        col_g, col_b, col_mixb, col_bi, col_bg, col_bso = (
            col(name) for name in ("ln_g", "ln_b", "mix_b", "bi", "bg", "bso"))
        col_mixw = col("mix_w").rearrange("p (f t) -> p f t", t=3)
        col_bsin = col("bsin_bd")[0:SD]
        col_bd = col("bsin_bd")[SD:P]
        col_bsel = col("bsel")[0:SD]
        w_sd, w_sel, w_i, w_g = (w_in[:, :, slice(*w_at[name])] for name in ("Wsin_Wd", "Wsel", "Wi", "Wg"))
        taps = sb("taps", [P, 18])
        w_so = sb("w_so", [SD, D])
        w_out = sb("w_out", [P, NF, D])
        k0_raw = sb("k0_raw", [P, 2 * NF, HID], U8)
        k1_raw = sb("k1_raw", [P, NH, HID], U8)
        k2_raw = sb("k2_raw", [P, NH, D], U8)
        w0 = sb("w0", [P, NF, HID], F16)
        w1 = sb("w1", [P, NH, HID], F16)
        w2 = sb("w2", [P, NH, D], F16)
        sgn = sb("sgn", [P, 3])
        w1_aff = sb("w1_aff", [P, 2])
        s_mag = sb("s_mag", [P, 3])
        s_all = sb("s_all", [P, 2])

        img = sb("img", [P, 2, C, 2, D])
        gray_a = sb("gray_a", [P, 2, D])
        gray_b = sb("gray_b", [P, 2, D])
        gray = sb("gray", [P, 2, 4, D + 2])
        edge = [sb(f"edge{c}", [P, 2, D]) for c in range(2)]
        edge_abs = [sb(f"edge_abs{c}", [P, 2, D]) for c in range(2)]
        h0 = sb("h0", [P, NT, D])
        st1 = sb("st1", [P, NT, 6])
        sum1 = sb("sum1", [P, NT, 2])
        dif1 = sb("dif1", [P, NT])
        sq1 = sb("sq1", [P, NT])
        mean1 = sb("mean1", [P, NT])
        dvar1 = sb("dvar1", [P, NT])
        var1 = sb("var1", [P, 2, NT])
        rs1 = sb("rs1", [P, 2, NT])
        rs1p = sb("rs1p", [P, NT])
        nmr = sb("nmr", [P, 2, 2, NT])
        norm = sb("norm", [P, NT, D])
        res = sb("res", [P, NT, D])
        hT = sb("hT", [P, NF, S + 2])
        mid = sb("mid", [P, NF, S])
        mixa = sb("mixa", [P, NF, S])
        mixT = sb("mixT", [P, NF, S])
        xs = sb("xs", [SD, S])
        dec = sb("dec", [SD, S])
        sel = sb("sel", [SD, S])
        nx = sb("nx", [SD, S])
        states = sb("states", [SD, S])
        selst = sb("selst", [SD, S])
        uT = sb("uT", [P, NF, S])
        gT = sb("gT", [P, NF, S])
        yu = sb("yu", [P, NF, S])
        gyu = sb("gyu", [P, NF, S])
        zT = sb("zT", [P, NF, S])
        h1 = sb("h1", [P, 2, NT, D])
        st2 = sb("st2", [P, NT, 6])
        sum2 = sb("sum2", [P, NT, 2])
        dif2 = sb("dif2", [P, NT])
        sq2 = sb("sq2", [P, NT])
        mean2 = sb("mean2", [P, NT])
        dvar2 = sb("dvar2", [P, NT])
        var2 = sb("var2", [P, NT])
        rs2 = sb("rs2", [P, NT])
        nmr2 = sb("nmr2", [P, NT])
        norm2 = sb("norm2", [P, NT, D])
        SW = S + 1
        x2h = sb("x2h", [P, NF, SW], F16)
        x2l = sb("x2l", [P, NF, SW], F16)
        r0h = sb("r0h", [P, NH, SW], F16)
        r0l = sb("r0l", [P, NH, SW], F16)
        r1h = sb("r1h", [P, NH, SW], F16)
        r1l = sb("r1l", [P, NH, SW], F16)
        outb = sb("outb", [P, NT, D])

        A = ctx.enter_context(nc.psum_tensor("psA", [P, 2, 512], F32))
        Bk = ctx.enter_context(nc.psum_tensor("psB", [P, 2, 512], F32))
        Q = [ctx.enter_context(nc.psum_tensor(f"psQ{i}", [P, 2, 512], F32)) for i in range(2)]

        LAYER1 = (Q[0], Q[1], Bk, Q[0])
        LAYER2 = (Q[1], Q[0], Q[1], Q[0])
        LAYER3 = Q[1]

        ld_row = sem("ld_row")
        ld_col = sem("ld_col")
        ld_win = sem("ld_win")
        ld_wout = sem("ld_wout")
        ld_k = [sem(f"ld_k{i}") for i in range(3)]
        cleared = sem("cleared")
        ident_set = sem("ident_set")
        prep = sem("prep")
        w0_part = sem("w0_part")
        tap_base = sem("tap_base")
        tap_mats = sem("tap_mats")
        first_init = sem("first_init")
        first_acc = sem("first_acc")
        first_conv = sem("first_conv")
        w_ready = [sem(f"w_ready{i}") for i in range(3)]
        ld_img = [sig(f"ld_img{par}", 1, 8, start=8 - 8 * par) for par in range(2)]
        ld_txt = sig("ld_txt", 1, 16)
        shifted = [sig(f"shifted{par}", 4, 8, start=32 - 32 * par) for par in range(2)]
        st_out = sig("st_out", 2, 16, start=16)
        gray_red = sig("gray_red", 1)
        edge_init = sig("edge_init", 2, start=-4)
        edge_abs_ok = sig("edge_abs_ok", 2)
        hT_ok = sig("hT_ok", 2 * NF)
        mid_ok = sig("mid_ok", NF)
        norm_ok = sig("norm_ok", NT)
        norm2_ok = sig("norm2_ok", NT)
        gates = sig("gates", 3)
        u_ok = sig("u_ok", NF)
        g_ok = sig("g_ok", NF)
        x2h_ok = sig("x2h_ok", 1)
        r0h_ok = sig("r0h_ok", NPAIR)
        r1h_ok = sig("r1h_ok", NPAIR)
        gray_sum = sig("gray_sum", 2)
        edge_acc = sig("edge_acc", 16, start=-32)
        tok_ok = sig("tok_ok", 1)
        ln1 = sig("ln1", NT + 9)
        res_ok = sig("res_ok", NT)
        mix = sig("mix", 2 * NF)
        state = sig("state", 3)
        yz = sig("yz", NF + 2)
        h1_ok = sig("h1_ok", NT)
        ln2 = sig("ln2", NT + 7)
        x2l_ok = sig("x2l_ok", 1)
        r0l_ok = sig("r0l_ok", NPAIR)
        r1l_ok = sig("r1l_ok", NPAIR)
        fin = sig("fin", 2, start=2)
        pow1 = sig("pow1", 1)
        pow2 = sig("pow2", 1)
        pe_t1 = sig("pe_t1", NF)
        pe_sd = sig("pe_sd", 2)
        pe_u = sig("pe_u", NF)
        pe_g = sig("pe_g", NF)
        pe_so = sig("pe_so", NF)
        pe_out = sig("pe_out", 2)
        pe_t2 = sig("pe_t2", 1)
        pe_f1 = sig("pe_f1", NPAIR)
        pe_f2 = sig("pe_f2", NPAIR)
        pe_f3 = sig("pe_f3", 2)

        def wait(eng, signal, batch, k):
            eng.wait_ge(signal.sem, signal.at(batch, k))

        def wait_before(eng, signal, batch):
            if not (isinstance(batch, int) and batch < 1):
                eng.wait_ge(signal.sem, signal.all_before(batch))

        block = ctx.enter_context(nc.Block())

        @block.sync
        def _(sp):
            def load_image(n, par):
                if not (isinstance(n, int) and n < 2):
                    wait(sp, gray_sum, n - 2, 2)
                sp.dma_start(img[:, par], x[n].rearrange("c (p j) w -> p c j w", j=2)).then_inc(ld_img[par].sem, 16)

            def load_text(n):
                wait_before(sp, res_ok, n)
                wait_before(sp, norm_ok, n)
                sp.dma_start(h0[0:TXT, 2], txt[n]).then_inc(ld_txt.sem, 16)

            def shift_rows(n, par):
                wait(sp, gray_sum, n, 2)
                lo, hi = 112, P - 1
                sp.dma_start(gray[1:1 + lo, par, 0, 1:D + 1], gray[0:lo, par, 2, 1:D + 1]).then_inc(shifted[par].sem, 16)
                sp.dma_start(gray[1 + lo:1 + hi, par, 0, 1:D + 1], gray[lo:hi, par, 2, 1:D + 1]).then_inc(shifted[par].sem, 16)
                sp.dma_start(gray[0:lo, par, 3, 1:D + 1], gray[1:1 + lo, par, 1, 1:D + 1]).then_inc(shifted[par].sem, 16)
                sp.dma_start(gray[lo:hi, par, 3, 1:D + 1], gray[1 + lo:1 + hi, par, 1, 1:D + 1]).then_inc(shifted[par].sem, 16)

            sp.dma_start(rows_all[:], row_pack.partition_broadcast(P)).then_inc(ld_row, 16)
            load_image(0, 0)
            sp.dma_start(cols[:], col_pack).then_inc(ld_col, 16)
            sp.wait_ge(cleared, 1)
            load_text(0)
            load_image(1, 1)
            sp.dma_start(w_in[:], w_pack.rearrange("(f p) n -> p f n", p=P)).then_inc(ld_win, 16)
            shift_rows(0, 0)
            shift_rows(1, 1)
            sp.dma_start(w_so[:], Wso).then_inc(ld_wout, 16)
            sp.dma_start(w_out[:], Wout.rearrange("(f p) n -> p f n", p=P)).then_inc(ld_wout, 16)
            for i, (raw, k) in enumerate(((k0_raw, k0), (k1_raw, k1), (k2_raw, k2))):
                sp.dma_start(raw[:], k.rearrange("(f p) n -> p f n", p=P)).then_inc(ld_k[i], 16)
            load_text(1)
            with sp.Fori(0, B - 3, 2) as b0:
                for par in range(2):
                    b = b0 + par
                    load_image(b + 2, par)
                    load_text(b + 2)
                    shift_rows(b + 2, par)

        @block.gpsimd
        def _(pool):
            nc.gpsimd.memset(h0[:, 2], 0.0).then_inc(cleared, 1)
            nc.gpsimd.memset(identw[:], 0.0).then_inc(ident_set, 1)
            pool.wait_ge(ident_set, 1)
            nc.gpsimd.affine_select(out=identw[:], in_=identw[:], compare_op=ALU.not_equal, fill=1.0, base=1,
                                    pattern=[[-1, P + 2]], channel_multiplier=1).then_inc(ident_set, 1)
            nc.gpsimd.memset(gray[:], 0.0).then_inc(cleared, 1)
            nc.gpsimd.memset(neg_half[:], -0.5).then_inc(cleared, 1)
            nc.gpsimd.memset(hT[:], 0.0).then_inc(cleared, 1)
            nc.gpsimd.memset(h1[:, :, 2], 0.0).then_inc(cleared, 1)
            pool.wait_ge(cleared, 5)

            def rsqrt1(n):
                wait(pool, ln1, n, NT + 7)
                nc.gpsimd.tensor_tensor(rs1[:].rearrange("p a t -> p (a t)"), var1[:].rearrange("p a t -> p (a t)"),
                                        neg_half[:], ALU.pow).then_inc(pow1.sem, 1)

            def rsqrt2(n):
                wait(pool, ln2, n, NT + 6)
                nc.gpsimd.tensor_tensor(rs2[:], var2[:], neg_half[:, 0:NT], ALU.pow).then_inc(pow2.sem, 1)

            rsqrt1(0)
            rsqrt1(1)
            rsqrt2(0)
            with pool.Fori(0, B - 3, 2) as b0:
                for par in range(2):
                    rsqrt1(b0 + par + 2)
                    rsqrt2(b0 + par + 1)
            rsqrt2(B - 1)

        @block.scalar
        def _(act):
            act_fn = nc.scalar.activation

            def gray_first(n, par):
                wait(act, ld_img[par], n, 1)
                act_fn(gray_a[:], img[:, par, 0], ACT.Copy, scale=GRAY[0]).then_inc(gray_red.sem, 1)

            def edge_first(n, par, c, done, dst):
                wait(act, gray_sum, n, 2)
                act_fn(dst[:], gray[:, par, 1:3, 0:D], ACT.Copy, scale=taps[:, 9 * c + 3:9 * c + 4]).then_inc(done, 1)

            def edge_fold(n):
                for c in range(2):
                    wait(act, edge_acc, n, 15 + c)
                    act_fn(edge_abs[c][:], edge[c][:], ACT.Abs).then_inc(edge_abs_ok.sem, 1)

            def edge_fold_first(n):
                act.wait_ge(first_conv, n + 1)
                act_fn(edge_abs[0][:].rearrange("p a b -> p (a b)"), Q[n][:, 0], ACT.Abs).then_inc(edge_abs_ok.sem, 1)
                act.wait_ge(first_acc, 8 * (n + 1))
                act_fn(edge_abs[1][:], edge[1 - n][:], ACT.Abs).then_inc(edge_abs_ok.sem, 1)

            def normalize(n, par):
                wait(act, ln1, n, NT + 8)
                for t in range(NT):
                    act_fn(norm[:, t], h0[:, t], ACT.Identity, scale=rs1[:, 1, t:t + 1],
                           bias=nmr[:, par, 1, t:t + 1]).then_inc(norm_ok.sem, 1)

            def normalize2(n, par):
                wait(act, ln2, n, NT + 7)
                for t in range(NT):
                    act_fn(norm2[:, t], h1[:, par, t], ACT.Identity, scale=rs2[:, t:t + 1],
                           bias=nmr2[:, t:t + 1]).then_inc(norm2_ok.sem, 1)

            def store(n):
                wait(act, fin, n, 1)
                act.dma_start(out[n, 0:H].rearrange("(p j) w -> p j w", j=2), outb[:, 0:2]).then_inc(st_out.sem, 16)
                wait(act, fin, n, 2)
                act.dma_start(out[n, H:S], outb[0:TXT, 2]).then_inc(st_out.sem, 16)

            def to_feature_major(n, f):
                if True:
                    wait(act, pe_t1, n, f + 1)
                    act_fn(hT[:, f, 1:1 + H].rearrange("q (p j) -> q j p", j=2),
                           A[:, f, 0:H].rearrange("q (j p) -> q j p", j=2), ACT.Identity,
                           scale=col_g[:, f:f + 1], bias=col_b[:, f:f + 1]).then_inc(hT_ok.sem, 1)
                    act_fn(hT[:, f, 1 + H:1 + S], A[:, f, H:S], ACT.Identity,
                           scale=col_g[:, f:f + 1], bias=col_b[:, f:f + 1]).then_inc(hT_ok.sem, 1)
                    wait(act, hT_ok, n, 2 * f + 2)
                    act_fn(mid[:, f], hT[:, f, 1:1 + S], ACT.Identity,
                           scale=col_mixw[:, f, 1:2], bias=col_mixb[:, f:f + 1]).then_inc(mid_ok.sem, 1)

            def gate_state(n):
                wait(act, pe_sd, n, 1)
                act_fn(dec[:], Bk[SD:P, 0, 0:S], ACT.Sigmoid, bias=col_bd).then_inc(gates.sem, 1)
                act_fn(xs[:], Bk[0:SD, 0, 0:S], ACT.Tanh, bias=col_bsin).then_inc(gates.sem, 1)
                wait(act, pe_sd, n, 2)
                act_fn(sel[:], Bk[0:SD, 1, 0:S], ACT.Sigmoid, bias=col_bsel).then_inc(gates.sem, 1)

            def gate_u(n):
                for f in range(NF):
                    wait(act, pe_u, n, f + 1)
                    act_fn(uT[:, f], A[:, f, 0:S], ACT.Tanh, bias=col_bi[:, f:f + 1]).then_inc(u_ok.sem, 1)

            def gate_g(n):
                for f in range(NF):
                    wait(act, pe_g, n, f + 1)
                    act_fn(gT[:, f], Bk[:, f, 0:S], ACT.Sigmoid, bias=col_bg[:, f:f + 1]).then_inc(g_ok.sem, 1)

            def x2_high(n):
                wait(act, pe_t2, n, 1)
                act_fn(x2h[:, :, 0:S], A[:, :, 0:S], ACT.Copy).then_inc(x2h_ok.sem, 1)

            def hidden_high(n, q, src, produced, dst, done):
                wait(act, produced, n, q + 1)
                act_fn(dst[:, 2 * q:2 * q + 2, 0:S], src[:, :, 0:S], ACT.Relu).then_inc(done.sem, 1)

            def h0_high(n, q):
                hidden_high(n, q, LAYER1[q], pe_f1, r0h, r0h_ok)

            def h1_high(n, q):
                hidden_high(n, q, LAYER2[q], pe_f2, r1h, r1h_ok)

            def step(b, par, mixer=True, tokens=True):
                n, t, other = b + 1, b + 2, 1 - par
                h0_high(b, 0)
                if tokens:
                    gray_first(t, par)
                h0_high(b, 1)
                h0_high(b, 2)
                if mixer:
                    to_feature_major(n, 0)
                h0_high(b, 3)
                if mixer:
                    to_feature_major(n, 1)
                if tokens:
                    edge_first(t, par, 0, edge_init.sem, edge[0])
                    edge_first(t, par, 1, edge_init.sem, edge[1])
                h1_high(b, 0)
                if mixer:
                    gate_state(n)
                    gate_u(n)
                    gate_g(n)
                h1_high(b, 1)
                if tokens:
                    edge_fold(t)
                h1_high(b, 2)
                if tokens:
                    normalize(t, par)
                if mixer:
                    normalize2(n, other)
                h1_high(b, 3)
                if mixer:
                    x2_high(n)
                store(b)

            def w1_convert(k):
                act_fn(w1[:, k], k1_raw[:, k], ACT.Identity, scale=w1_aff[:, 0:1], bias=w1_aff[:, 1:2]).then_inc(w_ready[1], 1)

            act.sem_inc(st_out.sem, st_out.start)
            act.wait_ge(prep, 1)
            act.wait_ge(ident_set, 2)
            for dy in range(3):
                for dx in range(3):
                    act_fn(tap_diag[:, dy, dx], ident, ACT.Copy,
                           scale=taps[:, 3 * dy + dx:3 * dy + dx + 1]).then_inc(tap_base, 1)
            gray_first(0, 0)
            edge_first(0, 0, 1, first_init, edge[1])
            gray_first(1, 1)
            edge_fold_first(0)
            edge_first(1, 1, 1, first_init, edge[0])
            normalize(0, 0)
            act.wait_ge(ld_col, 16)
            act.wait_ge(cleared, 5)
            for f in range(NF):
                to_feature_major(0, f)
            gate_state(0)
            gate_u(0)
            gate_g(0)
            edge_fold_first(1)
            act.wait_ge(prep, 5)
            act.wait_ge(ld_k[1], 16)
            for k in range(NH):
                w1_convert(k)
            normalize(1, 1)
            normalize2(0, 0)
            x2_high(0)
            with act.Fori(0, B - 3, 2) as b0:
                for par in range(2):
                    step(b0 + par, par)
            step(B - 2, 0, tokens=False)
            step(B - 1, 1, mixer=False, tokens=False)
            act.wait_ge(st_out.sem, st_out.at(B - 1, 2))

        @block.vector
        def _(dve):
            V = nc.vector

            def gray_rest(n, par):
                wait(dve, gray_red, n, 1)
                V.scalar_tensor_tensor(gray_b[:], img[:, par, 1], GRAY[1], gray_a[:], ALU.mult, ALU.add).then_inc(gray_sum.sem, 1)
                wait(dve, gray_sum, n, 1)
                V.scalar_tensor_tensor(gray[:, par, 1:3, 1:D + 1], img[:, par, 2], GRAY[2], gray_b[:], ALU.mult, ALU.add).then_inc(gray_sum.sem, 1)

            order = [(1, 1), (1, 2), (0, 0), (0, 1), (0, 2), (2, 0), (2, 1), (2, 2)]

            def edges(n, par, first, last):
                for k in range(first, last):
                    c, (dy, dx) = k % 2, order[k // 2]
                    if k < 2:
                        wait(dve, edge_init, n, k + 1)
                    else:
                        wait(dve, edge_acc, n, k - 1)
                    if k == 4:
                        wait(dve, shifted[par], n, 4)
                    tap = 9 * c + 3 * dy + dx
                    V.scalar_tensor_tensor(edge[c][:], gray[:, par, dy:dy + 2, dx:dx + D], taps[:, tap:tap + 1], edge[c][:],
                                           ALU.mult, ALU.add).then_inc(edge_acc.sem, 1)

            def edges_first(n, first, last):
                for k in range(first, last):
                    if k == 0:
                        dve.wait_ge(first_init, n + 1)
                    else:
                        dve.wait_ge(first_acc, 8 * n + k)
                    if k == 2:
                        wait(dve, shifted[n], n, 4)
                    dy, dx = order[k]
                    tap = 9 + 3 * dy + dx
                    V.scalar_tensor_tensor(edge[1 - n][:], gray[:, n, dy:dy + 2, dx:dx + D], taps[:, tap:tap + 1], edge[1 - n][:],
                                           ALU.mult, ALU.add).then_inc(first_acc, 1)

            def tokens_done(n):
                wait(dve, edge_abs_ok, n, 2)
                V.tensor_tensor(h0[:, 0:2], edge_abs[0][:], edge_abs[1][:], ALU.add).then_inc(tok_ok.sem, 1)

            def moments(n, done, st, total, dif, sq, mean, dvar):
                wait(dve, done, n, NT)
                V.tensor_tensor(total[:], st[:, :, 1:3], st[:, :, 4:6], ALU.add).then_inc(done.sem, 1)
                V.tensor_tensor(dif[:], st[:, :, 1], st[:, :, 4], ALU.subtract).then_inc(done.sem, 1)
                wait(dve, done, n, NT + 2)
                V.tensor_tensor(sq[:], dif[:], dif[:], ALU.mult).then_inc(done.sem, 1)
                V.tensor_scalar(mean[:], total[:, :, 0], 0.5, None, ALU.mult).then_inc(done.sem, 1)
                wait(dve, done, n, NT + 3)
                V.scalar_tensor_tensor(dvar[:], sq[:], D / 4, total[:, :, 1], ALU.mult, ALU.add).then_inc(done.sem, 1)
                wait(dve, done, n, NT + 5)

            def norm1_stats(n):
                wait(dve, ld_txt, n, 1)
                wait(dve, tok_ok, n, 1)
                for t in range(NT):
                    V.bn_stats(st1[:, t], h0[:, t]).then_inc(ln1.sem, 1)
                moments(n, ln1, st1, sum1, dif1, sq1, mean1, dvar1)
                V.tensor_scalar(var1[:, 0], dvar1[:], 1.0 / D, EPS, ALU.mult, ALU.add).then_inc(ln1.sem, 1)
                V.tensor_scalar(var1[:, 1], dvar1[:], (1.0 + EPS) / D, EPS * EPS, ALU.mult, ALU.add).then_inc(ln1.sem, 1)

            def norm1_bias(n, par):
                wait(dve, pow1, n, 1)
                V.scalar_tensor_tensor(nmr[:, par], mean1[:].unsqueeze(1).to_broadcast([P, 2, NT]), -1.0, rs1[:],
                                       ALU.mult, ALU.mult).then_inc(ln1.sem, 1)
                V.tensor_scalar(rs1p[:], rs1[:, 0], 1.0, None, ALU.add).then_inc(ln1.sem, 1)

            def norm1_residual(n):
                wait(dve, ln1, n, NT + 9)
                for t in range(NT):
                    V.scalar_tensor_tensor(res[:, t], h0[:, t], rs1p[:, t:t + 1], row_bout,
                                           ALU.mult, ALU.add).then_inc(res_ok.sem, 1)

            def mix_tokens(n, f):
                if True:
                    wait(dve, mid_ok, n, f + 1)
                    V.scalar_tensor_tensor(mixa[:, f], hT[:, f, 0:S], col_mixw[:, f, 0:1], mid[:, f],
                                           ALU.mult, ALU.add).then_inc(mix.sem, 1)
                    wait(dve, mix, n, 2 * f + 1)
                    V.scalar_tensor_tensor(mixT[:, f], hT[:, f, 2:S + 2], col_mixw[:, f, 2:3], mixa[:, f],
                                           ALU.mult, ALU.add).then_inc(mix.sem, 1)

            def scan_states(n):
                wait(dve, gates, n, 2)
                V.scalar_tensor_tensor(nx[:], dec[:], 1.0, xs[:], ALU.subtract, ALU.mult).then_inc(state.sem, 1)
                wait(dve, state, n, 1)
                V.tensor_tensor_scan(states[:], dec[:], nx[:], 0.0, ALU.mult, ALU.subtract).then_inc(state.sem, 1)
                wait(dve, gates, n, 3)
                wait(dve, state, n, 2)
                V.tensor_tensor(selst[:], states[:], sel[:], ALU.mult).then_inc(state.sem, 1)

            def blend(n):
                for f in range(NF):
                    wait(dve, pe_so, n, f + 1)
                    wait(dve, u_ok, n, f + 1)
                    V.scalar_tensor_tensor(yu[:, f], A[:, f, 0:S], col_bso[:, f:f + 1], uT[:, f],
                                           ALU.add, ALU.subtract).then_inc(yz.sem, 1)
                wait(dve, yz, n, NF)
                wait(dve, g_ok, n, NF)
                V.tensor_tensor(gyu[:], gT[:], yu[:], ALU.mult).then_inc(yz.sem, 1)
                wait(dve, yz, n, NF + 1)
                V.tensor_tensor(zT[:], gyu[:], uT[:], ALU.add).then_inc(yz.sem, 1)

            def residual(n, par):
                wait(dve, res_ok, n, NT)
                for t in range(NT):
                    if t != 1:
                        wait(dve, pe_out, n, t // 2 + 1)
                    rows = P if t < 2 else TXT
                    src = Bk[0:rows, t // 2, (t % 2) * D:(t % 2 + 1) * D]
                    V.scalar_tensor_tensor(h1[0:rows, par, t], src, nmr[0:rows, par, 0, t:t + 1], res[0:rows, t],
                                           ALU.add, ALU.add).then_inc(h1_ok.sem, 1)

            def norm2_stats(n, par):
                for t in range(NT):
                    wait(dve, h1_ok, n, t + 1)
                    V.bn_stats(st2[:, t], h1[:, par, t]).then_inc(ln2.sem, 1)
                moments(n, ln2, st2, sum2, dif2, sq2, mean2, dvar2)
                V.tensor_scalar(var2[:], dvar2[:], 1.0 / D, EPS, ALU.mult, ALU.add).then_inc(ln2.sem, 1)

            def norm2_bias(n):
                wait(dve, pow2, n, 1)
                V.scalar_tensor_tensor(nmr2[:], mean2[:], -1.0, rs2[:], ALU.mult, ALU.mult).then_inc(ln2.sem, 1)

            def x2_low(n):
                wait(dve, x2h_ok, n, 1)
                V.tensor_tensor(x2l[:, :, 0:S], A[:, :, 0:S], x2h[:, :, 0:S], ALU.subtract).then_inc(x2l_ok.sem, 1)

            def hidden_low(n, q, src, high_ok, high, dst, done):
                wait(dve, high_ok, n, q + 1)
                V.scalar_tensor_tensor(dst[:, 2 * q:2 * q + 2, 0:S], src[:, :, 0:S], 0.0,
                                       high[:, 2 * q:2 * q + 2, 0:S], ALU.max, ALU.subtract).then_inc(done.sem, 1)

            def h0_low(n, q):
                hidden_low(n, q, LAYER1[q], r0h_ok, r0h, r0l, r0l_ok)

            def h1_low(n, q):
                hidden_low(n, q, LAYER2[q], r1h_ok, r1h, r1l, r1l_ok)

            def finish(n, par):
                wait_before(dve, st_out, n)
                wait(dve, pe_f3, n, 1)
                V.scalar_tensor_tensor(outb[:, 0:2].rearrange("p t w -> p (t w)"), LAYER3[:, 0, 0:2 * D],
                                       s_all[:, 1:2], h1[:, par, 0:2].rearrange("p t w -> p (t w)"),
                                       ALU.mult, ALU.add).then_inc(fin.sem, 1)
                wait(dve, pe_f3, n, 2)
                V.scalar_tensor_tensor(outb[0:TXT, 2], LAYER3[0:TXT, 1, 0:D], s_all[0:TXT, 1:2],
                                       h1[0:TXT, par, 2], ALU.mult, ALU.add).then_inc(fin.sem, 1)

            def step(b, par, mixer=True, tokens=True):
                n, t, other = b + 1, b + 2, 1 - par
                h0_low(b, 0)
                if tokens:
                    gray_rest(t, par)
                h0_low(b, 1)
                h0_low(b, 2)
                if mixer:
                    mix_tokens(n, 0)
                h0_low(b, 3)
                if mixer:
                    mix_tokens(n, 1)
                if tokens:
                    edges(t, par, 0, 2)
                h1_low(b, 0)
                if tokens:
                    edges(t, par, 2, 3)
                if mixer:
                    scan_states(n)
                if tokens:
                    edges(t, par, 3, 15)
                h1_low(b, 1)
                if tokens:
                    edges(t, par, 15, 16)
                if mixer:
                    blend(n)
                if tokens:
                    tokens_done(t)
                    norm1_stats(t)
                h1_low(b, 2)
                if tokens:
                    norm1_bias(t, par)
                if mixer:
                    residual(n, other)
                    norm2_stats(n, other)
                if tokens:
                    norm1_residual(t)
                if mixer:
                    norm2_bias(n)
                h1_low(b, 3)
                if mixer:
                    x2_low(n)
                finish(b, par)

            dve.sem_inc(fin.sem, fin.start)
            dve.wait_ge(ld_row, 16)
            V.tensor_scalar(taps[:], taps_in, 0.5, None, ALU.mult).then_inc(prep, 1)
            V.tensor_scalar(sgn[:], s_in, 0.0, None, ALU.is_ge).then_inc(prep, 1)
            dve.wait_ge(prep, 2)
            V.tensor_scalar(sgn[:], sgn[:], 2.0, -1.0, ALU.mult, ALU.add).then_inc(prep, 1)
            dve.wait_ge(prep, 3)
            V.tensor_scalar(w1_aff[:, 0:1], sgn[:, 1:2], 2.0 * H2_SCALE, None, ALU.mult).then_inc(prep, 1)
            V.tensor_scalar(w1_aff[:, 1:2], sgn[:, 1:2], -H2_SCALE, None, ALU.mult).then_inc(prep, 1)
            V.tensor_tensor(s_mag[:], s_in, sgn[:], ALU.mult).then_inc(prep, 1)
            dve.wait_ge(prep, 6)
            V.scalar_tensor_tensor(s_all[:, 0:1], s_mag[:, 0:1], 8.0 / H2_SCALE, s_mag[:, 1:2], ALU.mult, ALU.mult).then_inc(prep, 1)
            dve.wait_ge(prep, 7)
            V.tensor_tensor(s_all[:, 1:2], s_all[:, 0:1], rows_all[:, row_at["s"][0] + 2:row_at["s"][1]], ALU.mult).then_inc(prep, 1)
            dve.wait_ge(ident_set, 2)
            for dx in range(3):
                dve.wait_ge(tap_base, 7 + dx)
                V.scalar_tensor_tensor(tap_up[:, dx], identw[:, 0:P], taps[:, dx:dx + 1], tap_diag[:, 2, dx],
                                       ALU.mult, ALU.add).then_inc(tap_mats, 1)
                V.scalar_tensor_tensor(tap_down[:, dx], identw[:, 2:P + 2], taps[:, 6 + dx:7 + dx], tap_diag[:, 0, dx],
                                       ALU.mult, ALU.add).then_inc(tap_mats, 1)
            dve.wait_ge(cleared, 5)
            gray_rest(0, 0)
            edges_first(0, 0, 2)
            gray_rest(1, 1)
            edges_first(0, 2, 8)
            tokens_done(0)
            norm1_stats(0)
            norm1_bias(0, 0)
            norm1_residual(0)
            edges_first(1, 0, 1)
            mix_tokens(0, 0)
            mix_tokens(0, 1)
            edges_first(1, 1, 4)
            scan_states(0)
            edges_first(1, 4, 8)
            blend(0)
            tokens_done(1)
            norm1_stats(1)
            dve.wait_ge(ld_k[0], 16)
            V.tensor_tensor(w0[:], k0_raw[:, 0:NF], k0_raw[:, NF:2 * NF], ALU.subtract).then_inc(w0_part, 1)
            residual(0, 0)
            norm1_bias(1, 1)
            norm2_stats(0, 0)
            dve.wait_ge(w0_part, 1)
            V.tensor_scalar(w0[:], w0[:], sgn[:, 0:1], None, ALU.mult).then_inc(w_ready[0], 1)
            norm2_bias(0)
            norm1_residual(1)
            dve.wait_ge(ld_k[2], 16)
            V.tensor_scalar(w2[:], k2_raw[:], 2.0, -1.0, ALU.mult, ALU.add).then_inc(w_ready[2], 1)
            x2_low(0)
            with dve.Fori(0, B - 3, 2) as b0:
                for par in range(2):
                    step(b0 + par, par)
            step(B - 2, 0, tokens=False)
            step(B - 1, 1, mixer=False, tokens=False)

        @block.tensor
        def _(pe):
            mm = nc.tensor.matmul

            def transposes(bank, f, src):
                for t in range(NT):
                    rows = P if t < 2 else TW
                    last = nc.tensor.transpose(bank[:, f, t * P:t * P + rows], src[0:rows, t, f * P:(f + 1) * P],
                                               ident[0:rows, 0:rows])
                return last

            def conv_first(n):
                wait(pe, gray_sum, n, 2)
                for out_slot in range(2):
                    for dx in range(3):
                        for in_slot in range(2):
                            if in_slot == out_slot:
                                m = tap_diag[:, 1, dx]
                            else:
                                m = tap_up[:, dx] if in_slot else tap_down[:, dx]
                            last = mm(Q[n][:, 0, out_slot * D:(out_slot + 1) * D], m, gray[:, n, 1 + in_slot, dx:dx + D],
                                      start=(dx == 0 and in_slot == 0), stop=(dx == 2 and in_slot == 1))
                last.then_inc(first_conv, 1)

            def transpose_norm1(n):
                for f in range(NF):
                    if f == 0:
                        wait(pe, norm_ok, n, NT)
                    transposes(A, f, norm).then_inc(pe_t1.sem, 1)

            def project(dst, w, lo, width):
                for k in range(NF):
                    last = mm(dst, w[:, k, lo:lo + width], mixT[:, k], start=(k == 0), stop=(k == NF - 1))
                return last

            def state_inputs(n):
                wait(pe, mix, n, 2 * NF)
                project(Bk[:, 0, 0:S], w_sd, 0, P).then_inc(pe_sd.sem, 1)
                project(Bk[0:SD, 1, 0:S], w_sel, 0, SD).then_inc(pe_sd.sem, 1)

            def u_inputs(n):
                for f in range(NF):
                    project(A[:, f, 0:S], w_i, f * P, P).then_inc(pe_u.sem, 1)

            def g_inputs(n):
                wait(pe, gates, n, 3)
                for f in range(NF):
                    project(Bk[:, f, 0:S], w_g, f * P, P).then_inc(pe_g.sem, 1)

            def state_output(n):
                wait(pe, state, n, 3)
                wait(pe, u_ok, n, NF)
                for f in range(NF):
                    mm(A[:, f, 0:S], w_so[:, f * P:(f + 1) * P], selst[:], start=True, stop=True).then_inc(pe_so.sem, 1)

            def mixer_output(n):
                wait(pe, yz, n, NF + 2)
                for t in range(NT):
                    rows = P if t < 2 else TXT
                    for k in range(NF):
                        lhs = zT[:, k, t:H:2] if t < 2 else zT[:, k, H:S]
                        last = mm(Bk[0:rows, t // 2, (t % 2) * D:(t % 2 + 1) * D], lhs, w_out[:, k],
                                  start=(k == 0), stop=(k == NF - 1))
                    if t > 0:
                        last.then_inc(pe_out.sem, 1)

            def transpose_norm2(n):
                wait(pe, norm2_ok, n, NT)
                for f in range(NF):
                    last = transposes(A, f, norm2)
                last.then_inc(pe_t2.sem, 1)

            def both(dst, lhs, k, high, low, first, last):
                mm(dst, lhs, high[:, k, 0:S], start=first, stop=False)
                return mm(dst, lhs, low[:, k, 0:S], start=False, stop=last)

            def layer1(n, q):
                if q == 0:
                    wait(pe, x2l_ok, n, 1)
                elif q == 3:
                    wait(pe, r0l_ok, n, 1)
                for m in range(2):
                    if q == 1 and not (isinstance(n, int) and n < 1):
                        wait(pe, fin, n - 1, m + 1)
                    if q == 2:
                        wait_before(pe, h1_ok, n + 1)
                    for k in range(NF):
                        col = (2 * q + m) * P
                        last = both(LAYER1[q][:, m, 0:S], w0[:, k, col:col + P], k, x2h, x2l,
                                    k == 0, k == NF - 1)
                last.then_inc(pe_f1.sem, 1)

            def layer2(n, q):
                if q == 0:
                    wait(pe, r0l_ok, n, 2)
                if q >= 2:
                    wait(pe, r1l_ok, n, q - 1)
                for ks in (range(0, NH - 2), range(NH - 2, NH)):
                    for m in range(2):
                        col = (2 * q + m) * P
                        for k in ks:
                            if q == 0 and m == 0 and k % 2 == 0:
                                wait(pe, r0l_ok, n, k // 2 + 1)
                            last = both(LAYER2[q][:, m, 0:S], w1[:, k, col:col + P], k, r0h, r0l,
                                        k == 0, k == NH - 1)
                last.then_inc(pe_f2.sem, 1)

            def layer3(n, tiles, ks):
                for t in tiles:
                    rows = P if t < 2 else TXT
                    dst = LAYER3[0:rows, t // 2, (t % 2) * D:(t % 2 + 1) * D]
                    for k in ks:
                        for part, r1 in enumerate((r1h, r1l)):
                            last = mm(dst, r1[:, k, t * P:t * P + rows], w2[:, k],
                                      start=(k == 0 and part == 0 and t != 1), stop=(k == NH - 1 and part == 1),
                                      skip_group_check=True)
                    if t > 0 and ks[-1] == NH - 1:
                        last.then_inc(pe_f3.sem, 1)

            def step(b, mixer=True):
                n = b + 1
                for q in range(NPAIR - 1):
                    layer1(b, q)
                if mixer:
                    transpose_norm1(n)
                layer1(b, NPAIR - 1)
                layer2(b, 0)
                if mixer:
                    state_inputs(n)
                    u_inputs(n)
                    g_inputs(n)
                layer2(b, 1)
                if mixer:
                    state_output(n)
                layer2(b, 2)
                if mixer:
                    mixer_output(n)
                layer2(b, 3)
                early, late = range(0, NH - 2), range(NH - 2, NH)
                wait(pe, r1l_ok, b, NPAIR - 1)
                layer3(b, range(2), early)
                if mixer:
                    transpose_norm2(n)
                layer3(b, range(2, NT), early)
                wait(pe, r1l_ok, b, NPAIR)
                layer3(b, range(NT), late)

            pe.wait_ge(ident_set, 2)
            pe.wait_ge(tap_mats, 6)
            conv_first(0)
            conv_first(1)
            transpose_norm1(0)
            pe.wait_ge(ld_win, 16)
            state_inputs(0)
            g_inputs(0)
            u_inputs(0)
            pe.wait_ge(ld_wout, 32)
            state_output(0)
            mixer_output(0)
            transpose_norm2(0)
            pe.wait_ge(w_ready[0], 1)
            pe.wait_ge(w_ready[1], NH)
            pe.wait_ge(w_ready[2], 1)
            with pe.Fori(0, B - 3, 2) as b0:
                for par in range(2):
                    step(b0 + par)
            step(B - 2)
            step(B - 1, mixer=False)


_AS_THEY_ARE = ['x', 'txt', 'L0_attn_Wso', 'L0_attn_Wout', 'L0_ffn_k0', 'L0_ffn_k1', 'L0_ffn_k2']


def kernel(**inputs):
    import numpy as _np
    import concourse.bacc as _bacc
    from concourse import mybir as _mybir
    from concourse.bass_utils import run_bass_kernel_spmd as _run

    def by_feature(v):
        v = _np.asarray(v)
        return v.reshape(2, P, -1).transpose(1, 0, 2).reshape(P, -1)

    a = {name.removeprefix('L0_attn_'): _np.asarray(v) for name, v in inputs.items()}
    half = a['bsel'].shape[0]
    packs = {
        'row_pack': _np.concatenate([a['L0_tok_scharr'].ravel()] + [a[f'L0_ffn_s{i}'].reshape(1) for i in range(3)]
                                    + [a['bout']]),
        'col_pack': _np.concatenate(
            [by_feature(a[n]) for n in ('ln_g', 'ln_b', 'mix_w', 'mix_b', 'bi', 'bg', 'bso')]
            + [_np.concatenate([a['bsin'], a['bd']]).reshape(P, 1), _np.resize(a['bsel'], P).reshape(P, 1)], axis=1),
        'w_pack': _np.concatenate([a[n] for n in ('Wsin', 'Wd', 'Wsel', 'Wi', 'Wg')], axis=1),
    }
    ordered = {n: inputs[n] for n in _AS_THEY_ARE[:2]} | packs | {n: inputs[n] for n in _AS_THEY_ARE[2:]}

    nc = _bacc.Bacc("TRN2", target_bir_lowering=False, num_devices=1)
    arrays, args = {}, []
    for name, v in ordered.items():
        v = _np.ascontiguousarray(v)
        arrays[f"in_{name}_dram"] = v
        args.append(nc.dram_tensor(f"in_{name}_dram", v.shape, _mybir.dt.from_np(v.dtype), kind="ExternalInput").ap())
    shape = (inputs['x'].shape[0], inputs['x'].shape[2] + inputs['txt'].shape[1], inputs['x'].shape[3])
    args.append(nc.dram_tensor("out_0_dram", shape, _mybir.dt.float32, kind="ExternalOutput").ap())
    early_fusion_kernel(nc, *args)
    r = _run(nc, [arrays], core_ids=[0])
    return r.results[0]["out_0_dram"]
```

```python
from contextlib import ExitStack

import concourse.bass as bass
from concourse import mybir

ALU = mybir.AluOpType
ACT = mybir.ActivationFunctionType
F32 = mybir.dt.float32
F16 = mybir.dt.float16
U8 = mybir.dt.uint8

P = 128
GRAY = (0.2989, 0.587, 0.114)
EPS = 1e-5


class Signal:

    def __init__(self, sem, per_batch, unit=1, start=0):
        self.sem, self.per_batch, self.unit, self.start = sem, per_batch, unit, start

    def at(self, batch, k):
        return batch * (self.per_batch * self.unit) + (k * self.unit + self.start)

    def all_before(self, batch):
        return self.at(batch, 0)


ROW_PARTS = (("scharr", 18), ("s", 3), ("bout", 256))
COL_PARTS = (("ln_g", 2), ("ln_b", 2), ("mix_w", 6), ("mix_b", 2), ("bi", 2), ("bg", 2), ("bso", 2),
             ("bsin_bd", 1), ("bsel", 1))
W_PARTS = (("Wsin_Wd", 128), ("Wsel", 64), ("Wi", 256), ("Wg", 256))


def spans(parts):
    at, found = 0, {}
    for name, width in parts:
        found[name] = (at, at + width)
        at += width
    return found, at


def early_fusion_kernel(nc, x, txt, row_pack, col_pack, w_pack, Wso, Wout, k0, k1, k2, out):
    B, C, H, D = x.shape
    TXT = txt.shape[1]
    S = H + TXT
    SD = Wso.shape[0]
    HID = k0.shape[1]
    NF = D // P
    NH = HID // P
    NT = 3
    TW = TXT + 1
    NPAIR = NH // 2
    SEL_TOKENS = ((0, S // 2 + 1), (S // 2 + 1, S))
    assert H == 2 * P and D == 2 * P and SD == P // 2 and TXT < P and S <= 512 and B % 2 == 0
    H2_SCALE = 0.125

    with ExitStack() as ctx:
        def sb(name, shape, dt=F32):
            return ctx.enter_context(nc.sbuf_tensor(name, shape, dt))

        def sem(name):
            return ctx.enter_context(nc.semaphore(name))

        def sig(name, per_batch, unit=1, start=0):
            return Signal(sem(name), per_batch, unit, start)

        identw = sb("identw", [P, P + 2])
        ident = identw[:, 1:P + 1]
        tap_diag = sb("tap_diag", [P, 2, 3, 3, P])
        tap_up = sb("tap_up", [P, 2, 3, P])
        tap_down = sb("tap_down", [P, 2, 3, P])
        neg_half = sb("neg_half", [P, NT])
        row_at, row_width = spans(ROW_PARTS)
        col_at, col_width = spans(COL_PARTS)
        w_at, w_width = spans(W_PARTS)
        rows_all = sb("rows_all", [P, row_width])
        cols = sb("cols", [P, col_width])
        w_in = sb("w_in", [P, NF, w_width])

        def col(name):
            return cols[:, slice(*col_at[name])]

        taps_in = rows_all[:, slice(*row_at["scharr"])]
        s_in = rows_all[:, slice(*row_at["s"])]
        row_bout = rows_all[:, slice(*row_at["bout"])]
        col_g, col_b, col_mixb, col_bi, col_bg, col_bso = (
            col(name) for name in ("ln_g", "ln_b", "mix_b", "bi", "bg", "bso"))
        col_mixw = col("mix_w").rearrange("p (f t) -> p f t", t=3)
        col_bsin = col("bsin_bd")[0:SD]
        col_bd = col("bsin_bd")[SD:P]
        col_bsel = col("bsel")
        w_sd, w_sel, w_i, w_g = (w_in[:, :, slice(*w_at[name])] for name in ("Wsin_Wd", "Wsel", "Wi", "Wg"))
        taps = sb("taps", [P, 18])
        w_so = sb("w_so", [P, P])
        w_out = sb("w_out", [P, NF, D])
        k0_raw = sb("k0_raw", [P, 2 * NF, HID], U8)
        k1_raw = sb("k1_raw", [P, NH, HID], U8)
        k2_raw = sb("k2_raw", [P, NH, D], U8)
        w0 = sb("w0", [P, NF, HID], F16)
        w1 = sb("w1", [P, NH, HID], F16)
        w2 = sb("w2", [P, NH, D], F16)
        sgn = sb("sgn", [P, 3])
        w1_aff = sb("w1_aff", [P, 2])
        s_mag = sb("s_mag", [P, 3])
        s_all = sb("s_all", [P, 2])

        img = sb("img", [P, 2, C, 2, D])
        gray_a = sb("gray_a", [P, 2, D])
        gray_b = sb("gray_b", [P, 2, D])
        gray = sb("gray", [P, 2, 4, D + 2])
        edge = [sb(f"edge{c}", [P, 2, D]) for c in range(2)]
        edge_abs = [sb(f"edge_abs{c}", [P, 2, D]) for c in range(2)]
        h0 = sb("h0", [P, NT, D])
        st1 = sb("st1", [P, NT, 6])
        mom1 = sb("mom1", [P, NT, 2])
        sum1 = sb("sum1", [P, NT, 2])
        dif1 = sb("dif1", [P, NT])
        sq1 = sb("sq1", [P, NT])
        var1 = sb("var1", [P, 2, NT])
        rs1 = sb("rs1", [P, 2, NT])
        rs1p = sb("rs1p", [P, NT])
        nmr = sb("nmr", [P, 2, 2, NT])
        norm = sb("norm", [P, NT, D])
        res = sb("res", [P, NT, D])
        hT = sb("hT", [P, NF, S + 2])
        mid = sb("mid", [P, NF, S])
        mixa = sb("mixa", [P, NF, S])
        mixT = sb("mixT", [P, NF, S])
        xs = sb("xs", [SD, S])
        dec = sb("dec", [SD, S])
        sel = sb("sel", [SD, S])
        nx = sb("nx", [SD, S])
        states = sb("states", [SD, S])
        selst = sb("selst", [P, S])
        uT = sb("uT", [P, NF, S])
        gT = sb("gT", [P, NF, S])
        yu = sb("yu", [P, NF, S])
        gyu = sb("gyu", [P, NF, S])
        zT = sb("zT", [P, NF, S])
        h1 = sb("h1", [P, 2, NT, D])
        st2 = sb("st2", [P, NT, 6])
        mom2 = sb("mom2", [P, NT, 2])
        sum2 = sb("sum2", [P, NT, 2])
        dif2 = sb("dif2", [P, NT])
        sq2 = sb("sq2", [P, NT])
        var2 = sb("var2", [P, NT])
        rs2 = sb("rs2", [P, NT])
        nmr2 = sb("nmr2", [P, NT])
        norm2 = sb("norm2", [P, NT, D])
        SW = S + 1
        x2h = sb("x2h", [P, NF, SW], F16)
        x2l = sb("x2l", [P, NF, SW], F16)
        r0h = sb("r0h", [P, NH, SW], F16)
        r0l = sb("r0l", [P, NH, SW], F16)
        r1h = sb("r1h", [P, NH, SW], F16)
        r1l = sb("r1l", [P, NH, SW], F16)
        outb = sb("outb", [P, NT, D])

        A = ctx.enter_context(nc.psum_tensor("psA", [P, 2, 512], F32))
        Bk = ctx.enter_context(nc.psum_tensor("psB", [P, 2, 512], F32))
        Q = [ctx.enter_context(nc.psum_tensor(f"psQ{i}", [P, 2, 512], F32)) for i in range(2)]

        RESIDUAL_ORDER = (2, 0, 1)
        LAYER1 = (Q[0], Q[1], Bk, Q[0])
        LAYER2 = (Q[1], Q[0], Q[1], Q[0])
        LAYER3 = Q[1]

        ld_row = sem("ld_row")
        ld_col = sem("ld_col")
        ld_colour = [sem(f"ld_colour{c}") for c in range(3)]
        ld_win = sem("ld_win")
        ld_wout = sem("ld_wout")
        ld_k = [sem(f"ld_k{i}") for i in range(3)]
        cleared = sem("cleared")
        ident_set = sem("ident_set")
        prep = sem("prep")
        w0_part = sem("w0_part")
        tap_diag0 = sem("tap_diag0")
        tap_outer = sem("tap_outer")
        tap_diag1 = sem("tap_diag1")
        tap_mats = [sem(f"tap_mats{c}") for c in range(2)]
        first_rows = sem("first_rows")
        first_shift = sem("first_shift")
        first_init = sem("first_init")
        first_acc = sem("first_acc")
        first_conv = sem("first_conv")
        w_ready = [sem(f"w_ready{i}") for i in range(3)]
        ld_img = [sig(f"ld_img{par}", 1, 8, start=-8 * (1 - par)) for par in range(2)]
        ld_txt = sig("ld_txt", 1, 16)
        shifted = [sig(f"shifted{par}", 4, 8, start=-32 - 32 * par) for par in range(2)]
        st_out = sig("st_out", 2, 16, start=16)
        gray_red = sig("gray_red", 1)
        edge_init = sig("edge_init", 2, start=-4)
        edge_abs_ok = sig("edge_abs_ok", 2)
        hT_ok = sig("hT_ok", 2 * NF)
        mid_ok = sig("mid_ok", NF)
        norm_ok = sig("norm_ok", NT)
        norm2_ok = sig("norm2_ok", NT)
        gates = sig("gates", 4)
        u_ok = sig("u_ok", NF)
        g_ok = sig("g_ok", NF)
        x2h_ok = sig("x2h_ok", NF)
        r0h_ok = sig("r0h_ok", NPAIR)
        r1h_ok = sig("r1h_ok", NPAIR)
        gray_sum = sig("gray_sum", 2)
        edge_acc = sig("edge_acc", 16, start=-32)
        tok_ok = sig("tok_ok", 1)
        ln1 = sig("ln1", NT + 10)
        res_ok = sig("res_ok", NT)
        mix_a = sig("mix_a", NF)
        mix = sig("mix", NF)
        state = sig("state", 4)
        yz = sig("yz", 3 * NF)
        h1_ok = sig("h1_ok", NT)
        ln2 = sig("ln2", NT + 7)
        x2l_ok = sig("x2l_ok", NF)
        r0l_ok = sig("r0l_ok", NPAIR)
        r1l_ok = sig("r1l_ok", NPAIR)
        fin = sig("fin", 2, start=2)
        pow1 = sig("pow1", 2)
        pow2 = sig("pow2", 1)
        pe_t1 = sig("pe_t1", NF)
        pe_sd = sig("pe_sd", 3)
        pe_u = sig("pe_u", NF)
        pe_g = sig("pe_g", NF)
        pe_so = sig("pe_so", NF)
        pe_out = sig("pe_out", 2)
        pe_t2 = sig("pe_t2", NF)
        pe_f1 = sig("pe_f1", NPAIR)
        pe_f2 = sig("pe_f2", NPAIR)
        pe_f3 = sig("pe_f3", 2)

        def wait(eng, signal, batch, k):
            eng.wait_ge(signal.sem, signal.at(batch, k))

        def wait_before(eng, signal, batch):
            if not (isinstance(batch, int) and batch < 1):
                eng.wait_ge(signal.sem, signal.all_before(batch))

        block = ctx.enter_context(nc.Block())

        @block.sync
        def _(sp):
            def load_image(n, par):
                if not (isinstance(n, int) and n < 2):
                    wait(sp, gray_sum, n - 2, 2)
                sp.dma_start(img[:, par], x[n].rearrange("c (p j) w -> p c j w", j=2)).then_inc(ld_img[par].sem, 16)

            def load_text(n):
                wait_before(sp, res_ok, n)
                wait_before(sp, norm_ok, n)
                sp.dma_start(h0[0:TXT, 2], txt[n]).then_inc(ld_txt.sem, 16)

            def shift_rows(n, par):
                wait(sp, gray_sum, n, 2)
                lo, hi = 112, P - 1
                sp.dma_start(gray[1:1 + lo, par, 0, 1:D + 1], gray[0:lo, par, 2, 1:D + 1]).then_inc(shifted[par].sem, 16)
                sp.dma_start(gray[1 + lo:1 + hi, par, 0, 1:D + 1], gray[lo:hi, par, 2, 1:D + 1]).then_inc(shifted[par].sem, 16)
                sp.dma_start(gray[0:lo, par, 3, 1:D + 1], gray[1:1 + lo, par, 1, 1:D + 1]).then_inc(shifted[par].sem, 16)
                sp.dma_start(gray[lo:hi, par, 3, 1:D + 1], gray[1 + lo:1 + hi, par, 1, 1:D + 1]).then_inc(shifted[par].sem, 16)

            def store(n):
                wait(sp, fin, n, 1)
                sp.dma_start(out[n, 0:H].rearrange("(p j) w -> p j w", j=2), outb[:, 0:2]).then_inc(st_out.sem, 16)
                wait(sp, fin, n, 2)
                sp.dma_start(out[n, H:S], outb[0:TXT, 2]).then_inc(st_out.sem, 16)

            def step(b, par, image=True):
                load_text(b + 2)
                shift_rows(b + 2, par)
                if image:
                    load_image(b + 3, 1 - par)
                store(b)

            sp.sem_inc(st_out.sem, st_out.start)
            sp.dma_start(rows_all[:], row_pack.partition_broadcast(P)).then_inc(ld_row, 16)
            for c in range(3):
                sp.dma_start(img[:, 0, c], x[0, c].rearrange("(p j) w -> p j w", j=2)).then_inc(ld_colour[c], 16)
            sp.dma_start(cols[:], col_pack).then_inc(ld_col, 16)
            sp.wait_ge(cleared, 1)
            load_text(0)
            load_image(1, 1)
            sp.dma_start(w_in[:], w_pack.rearrange("(f p) n -> p f n", p=P)).then_inc(ld_win, 16)
            for f in range(NF):
                sp.dma_start(w_so[f * SD:(f + 1) * SD], Wso[:, f * P:(f + 1) * P]).then_inc(ld_wout, 16)
            sp.dma_start(w_out[:], Wout.rearrange("(f p) n -> p f n", p=P)).then_inc(ld_wout, 16)
            for i, (raw, k) in enumerate(((k0_raw, k0), (k1_raw, k1), (k2_raw, k2))):
                sp.dma_start(raw[:], k.rearrange("(f p) n -> p f n", p=P)).then_inc(ld_k[i], 16)
            load_text(1)
            load_image(2, 0)
            with sp.Fori(0, B - 5, 2) as b0:
                for par in range(2):
                    step(b0 + par, par)
            step(B - 4, 0)
            step(B - 3, 1, image=False)
            store(B - 2)
            store(B - 1)
            sp.wait_ge(st_out.sem, st_out.at(B - 1, 2))

        @block.gpsimd
        def _(pool):
            nc.gpsimd.memset(h0[:, 2], 0.0).then_inc(cleared, 1)
            nc.gpsimd.memset(identw[:], 0.0).then_inc(ident_set, 1)
            pool.wait_ge(ident_set, 1)
            nc.gpsimd.affine_select(out=identw[:], in_=identw[:], compare_op=ALU.not_equal, fill=1.0, base=1,
                                    pattern=[[-1, P + 2]], channel_multiplier=1).then_inc(ident_set, 1)
            nc.gpsimd.memset(gray[:], 0.0).then_inc(cleared, 1)
            nc.gpsimd.memset(neg_half[:], -0.5).then_inc(cleared, 1)
            nc.gpsimd.memset(hT[:], 0.0).then_inc(cleared, 1)
            nc.gpsimd.memset(h1[:, :, 2], 0.0).then_inc(cleared, 1)
            pool.wait_ge(cleared, 5)

            def rsqrt1(n):
                wait(pool, ln1, n, NT + 7)
                for form in (1, 0):
                    nc.gpsimd.tensor_tensor(rs1[:, form], var1[:, form], neg_half[:], ALU.pow).then_inc(pow1.sem, 1)

            def rsqrt2(n):
                wait(pool, ln2, n, NT + 6)
                nc.gpsimd.tensor_tensor(rs2[:], var2[:], neg_half[:], ALU.pow).then_inc(pow2.sem, 1)

            rsqrt1(0)
            rsqrt2(0)
            rsqrt1(1)
            with pool.Fori(0, B - 3, 2) as b0:
                for par in range(2):
                    rsqrt1(b0 + par + 2)
                    rsqrt2(b0 + par + 1)
            rsqrt2(B - 1)

        @block.scalar
        def _(act):
            act_fn = nc.scalar.activation

            def gray_first(n, par):
                if isinstance(n, int) and n == 0:
                    act.wait_ge(ld_colour[0], 16)
                else:
                    wait(act, ld_img[par], n, 1)
                act_fn(gray_a[:], img[:, par, 0], ACT.Copy, scale=GRAY[0]).then_inc(gray_red.sem, 1)

            def edge_first(n, par, c, done, dst):
                wait(act, gray_sum, n, 2)
                act_fn(dst[:], gray[:, par, 1:3, 0:D], ACT.Copy, scale=taps[:, 9 * c + 3:9 * c + 4]).then_inc(done, 1)

            def edge_fold(n):
                for c in range(2):
                    wait(act, edge_acc, n, 15 + c)
                    act_fn(edge_abs[c][:], edge[c][:], ACT.Abs).then_inc(edge_abs_ok.sem, 1)

            def edge_fold_first(n):
                for c in range(2):
                    if (n, c) == (0, 1):
                        act.wait_ge(first_acc, 8)
                        src = edge[1][:].rearrange("p a b -> p (a b)")
                    else:
                        act.wait_ge(first_conv, 2 * (1 + n + c))
                        src = Q[n][:, c]
                    act_fn(edge_abs[c][:].rearrange("p a b -> p (a b)"), src, ACT.Abs).then_inc(edge_abs_ok.sem, 1)

            def normalize(n, par):
                wait(act, ln1, n, NT + 8)
                for t in range(NT):
                    act_fn(norm[:, t], h0[:, t], ACT.Identity, scale=rs1[:, 1, t:t + 1],
                           bias=nmr[:, par, 1, t:t + 1]).then_inc(norm_ok.sem, 1)

            def normalize2(n, par):
                wait(act, ln2, n, NT + 7)
                for t in range(NT):
                    act_fn(norm2[:, t], h1[:, par, t], ACT.Identity, scale=rs2[:, t:t + 1],
                           bias=nmr2[:, t:t + 1]).then_inc(norm2_ok.sem, 1)

            def to_feature_major(n, f):
                wait(act, pe_t1, n, f + 1)
                act_fn(hT[:, f, 1:1 + H].rearrange("q (p j) -> q j p", j=2),
                       A[:, f, 0:H].rearrange("q (j p) -> q j p", j=2), ACT.Identity,
                       scale=col_g[:, f:f + 1], bias=col_b[:, f:f + 1]).then_inc(hT_ok.sem, 1)
                act_fn(hT[:, f, 1 + H:1 + S], A[:, f, H:S], ACT.Identity,
                       scale=col_g[:, f:f + 1], bias=col_b[:, f:f + 1]).then_inc(hT_ok.sem, 1)

            def middle_tap(n, f):
                wait(act, hT_ok, n, 2 * f + 2)
                act_fn(mid[:, f], hT[:, f, 1:1 + S], ACT.Identity,
                       scale=col_mixw[:, f, 1:2], bias=col_mixb[:, f:f + 1]).then_inc(mid_ok.sem, 1)

            def gate_state(n):
                wait(act, pe_sd, n, 1)
                act_fn(dec[:], Bk[SD:P, 0, 0:S], ACT.Sigmoid, bias=col_bd).then_inc(gates.sem, 1)
                act_fn(xs[:], Bk[0:SD, 0, 0:S], ACT.Tanh, bias=col_bsin).then_inc(gates.sem, 1)
                for half, (lo, hi) in enumerate(SEL_TOKENS):
                    wait(act, pe_sd, n, 2 + half)
                    rows = slice(half * SD, (half + 1) * SD)
                    act_fn(sel[:, lo:hi], Bk[rows, 1, 0:hi - lo], ACT.Sigmoid, bias=col_bsel[rows]).then_inc(gates.sem, 1)

            def gate_u(n):
                for f in range(NF):
                    wait(act, pe_u, n, f + 1)
                    act_fn(uT[:, f], A[:, f, 0:S], ACT.Tanh, bias=col_bi[:, f:f + 1]).then_inc(u_ok.sem, 1)

            def gate_g(n, bank=Bk):
                for f in range(NF):
                    wait(act, pe_g, n, f + 1)
                    act_fn(gT[:, f], bank[:, f, 0:S], ACT.Sigmoid, bias=col_bg[:, f:f + 1]).then_inc(g_ok.sem, 1)

            def x2_high(n):
                for f in range(NF):
                    wait(act, pe_t2, n, f + 1)
                    act_fn(x2h[:, f, 0:S], A[:, f, 0:S], ACT.Copy).then_inc(x2h_ok.sem, 1)

            def hidden_high(n, q, src, produced, dst, done):
                wait(act, produced, n, q + 1)
                act_fn(dst[:, 2 * q:2 * q + 2, 0:S], src[:, :, 0:S], ACT.Relu).then_inc(done.sem, 1)

            def h0_high(n, q):
                hidden_high(n, q, LAYER1[q], pe_f1, r0h, r0h_ok)

            def h1_high(n, q):
                hidden_high(n, q, LAYER2[q], pe_f2, r1h, r1h_ok)

            def step(b, par, mixer=True, tokens=True):
                n, t, other = b + 1, b + 2, 1 - par
                h0_high(b, 0)
                h0_high(b, 1)
                if tokens:
                    gray_first(t, par)
                h0_high(b, 2)
                if mixer:
                    to_feature_major(n, 0)
                    middle_tap(n, 0)
                h0_high(b, 3)
                if mixer:
                    to_feature_major(n, 1)
                    middle_tap(n, 1)
                if tokens:
                    edge_first(t, par, 0, edge_init.sem, edge[0])
                    edge_first(t, par, 1, edge_init.sem, edge[1])
                h1_high(b, 0)
                if mixer:
                    gate_state(n)
                    gate_u(n)
                    gate_g(n)
                h1_high(b, 1)
                if tokens:
                    edge_fold(t)
                h1_high(b, 2)
                if mixer:
                    normalize2(n, other)
                h1_high(b, 3)
                if mixer:
                    x2_high(n)
                if tokens:
                    normalize(t, par)

            def w1_convert(first, last):
                for k in range(first, last):
                    act_fn(w1[:, k], k1_raw[:, k], ACT.Identity, scale=w1_aff[:, 0:1], bias=w1_aff[:, 1:2]).then_inc(w_ready[1], 1)

            def diagonal(c, dy, dx, done):
                tap = 9 * c + 3 * dy + dx
                act_fn(tap_diag[:, c, dy, dx], ident, ACT.Copy, scale=taps[:, tap:tap + 1]).then_inc(done, 1)

            act.wait_ge(prep, 1)
            act.wait_ge(ident_set, 2)
            for dx in range(3):
                diagonal(0, 2, dx, tap_diag0)
            gray_first(0, 0)
            for dx in range(3):
                diagonal(0, 1, dx, tap_diag0)
            edge_first(0, 0, 1, first_init, edge[1])
            gray_first(1, 1)
            act.wait_ge(first_rows, 1)
            for slot in range(2):
                act_fn(gray[:, 0, 3 * slot, 1:D + 1], Q[0][:, 1, slot * D:(slot + 1) * D], ACT.Copy).then_inc(first_shift, 1)
            for dy in range(3):
                for dx in range(3):
                    diagonal(1, dy, dx, tap_diag1)
            edge_fold_first(0)
            act.wait_ge(prep, 5)
            act.wait_ge(ld_k[1], 16)
            w1_convert(0, 2)
            act.wait_ge(ld_col, 16)
            act.wait_ge(cleared, 5)
            for f in range(NF):
                to_feature_major(0, f)
            edge_fold_first(1)
            gate_state(0)
            gate_u(0)
            gate_g(0, Q[0])
            w1_convert(2, NH)
            x2_high(0)
            normalize(1, 1)
            with act.Fori(0, B - 3, 2) as b0:
                for par in range(2):
                    step(b0 + par, par)
            step(B - 2, 0, tokens=False)
            step(B - 1, 1, mixer=False, tokens=False)

        @block.vector
        def _(dve):
            V = nc.vector

            def gray_green(n, par):
                wait(dve, gray_red, n, 1)
                V.scalar_tensor_tensor(gray_b[:], img[:, par, 1], GRAY[1], gray_a[:], ALU.mult, ALU.add).then_inc(gray_sum.sem, 1)

            def gray_blue(n, par):
                wait(dve, gray_sum, n, 1)
                V.scalar_tensor_tensor(gray[:, par, 1:3, 1:D + 1], img[:, par, 2], GRAY[2], gray_b[:], ALU.mult, ALU.add).then_inc(gray_sum.sem, 1)

            order = [(1, 1), (1, 2), (0, 0), (0, 1), (0, 2), (2, 0), (2, 1), (2, 2)]

            def edges(n, par, first, last):
                for k in range(first, last):
                    c, (dy, dx) = k % 2, order[k // 2]
                    if k < 2:
                        wait(dve, edge_init, n, k + 1)
                    else:
                        wait(dve, edge_acc, n, k - 1)
                    if k == 4:
                        wait(dve, shifted[par], n, 4)
                    tap = 9 * c + 3 * dy + dx
                    V.scalar_tensor_tensor(edge[c][:], gray[:, par, dy:dy + 2, dx:dx + D], taps[:, tap:tap + 1], edge[c][:],
                                           ALU.mult, ALU.add).then_inc(edge_acc.sem, 1)

            def edge_first(k):
                if k == 0:
                    dve.wait_ge(first_init, 1)
                else:
                    dve.wait_ge(first_acc, k)
                if k == 2:
                    dve.wait_ge(first_shift, 2)
                dy, dx = order[k]
                tap = 9 + 3 * dy + dx
                V.scalar_tensor_tensor(edge[1][:], gray[:, 0, dy:dy + 2, dx:dx + D], taps[:, tap:tap + 1], edge[1][:],
                                       ALU.mult, ALU.add).then_inc(first_acc, 1)

            def tap_matrices(c, to_slot):
                shift, matrices, dy_ident, dy_diag = ((0, tap_up, 0, 2), (2, tap_down, 2, 0))[to_slot]
                for dx in range(3):
                    tap = 9 * c + 3 * dy_ident + dx
                    V.scalar_tensor_tensor(matrices[:, c, dx], identw[:, shift:shift + P], taps[:, tap:tap + 1],
                                           tap_diag[:, c, dy_diag, dx], ALU.mult, ALU.add).then_inc(tap_mats[c], 1)

            def tokens_done(n):
                wait(dve, edge_abs_ok, n, 2)
                V.tensor_tensor(h0[:, 0:2], edge_abs[0][:], edge_abs[1][:], ALU.add).then_inc(tok_ok.sem, 1)

            def moments(n, done, st, total, dif, sq, mom):
                wait(dve, done, n, NT)
                V.tensor_tensor(total[:], st[:, :, 1:3], st[:, :, 4:6], ALU.add).then_inc(done.sem, 1)
                V.tensor_tensor(dif[:], st[:, :, 1], st[:, :, 4], ALU.subtract).then_inc(done.sem, 1)
                wait(dve, done, n, NT + 2)
                V.tensor_tensor(sq[:], dif[:], dif[:], ALU.mult).then_inc(done.sem, 1)
                V.tensor_scalar(mom[:, :, 0], total[:, :, 0], 0.5, None, ALU.mult).then_inc(done.sem, 1)
                wait(dve, done, n, NT + 3)
                V.scalar_tensor_tensor(mom[:, :, 1], sq[:], D / 4, total[:, :, 1], ALU.mult, ALU.add).then_inc(done.sem, 1)
                wait(dve, done, n, NT + 5)

            def moments_first(n, done, st, mom):
                wait(dve, done, n, NT)
                for t in range(NT):
                    V.bn_aggr(mom[:, t], st[:, t]).then_inc(done.sem, 2 if t else 1)
                wait(dve, done, n, NT + 5)

            def norm1_stats(n):
                wait(dve, ld_txt, n, 1)
                for t in (2, 0, 1):
                    if t == 0:
                        wait(dve, tok_ok, n, 1)
                    V.bn_stats(st1[:, t], h0[:, t]).then_inc(ln1.sem, 1)

            def norm1_variances(n, count):
                V.tensor_scalar(var1[:, 1], mom1[:, :, 1], (1.0 + EPS) / count, EPS * EPS, ALU.mult, ALU.add).then_inc(ln1.sem, 1)
                V.tensor_scalar(var1[:, 0], mom1[:, :, 1], 1.0 / count, EPS, ALU.mult, ALU.add).then_inc(ln1.sem, 1)

            def norm1_bias(n, par):
                wait(dve, pow1, n, 1)
                V.scalar_tensor_tensor(nmr[:, par, 1], mom1[:, :, 0], -1.0, rs1[:, 1], ALU.mult, ALU.mult).then_inc(ln1.sem, 1)

            def residual_bias(n, par):
                wait(dve, pow1, n, 2)
                V.scalar_tensor_tensor(nmr[:, par, 0], mom1[:, :, 0], -1.0, rs1[:, 0], ALU.mult, ALU.mult).then_inc(ln1.sem, 1)
                V.tensor_scalar(rs1p[:], rs1[:, 0], 1.0, None, ALU.add).then_inc(ln1.sem, 1)

            def normalize_first(n):
                wait(dve, ln1, n, NT + 8)
                for t in range(NT):
                    V.tensor_scalar(norm[:, t], h0[:, t], rs1[:, 1, t:t + 1], nmr[:, 0, 1, t:t + 1],
                                    ALU.mult, ALU.add).then_inc(norm_ok.sem, 1)

            def norm1_residual(n):
                wait(dve, ln1, n, NT + 10)
                for t in range(NT):
                    V.scalar_tensor_tensor(res[:, t], h0[:, t], rs1p[:, t:t + 1], row_bout,
                                           ALU.mult, ALU.add).then_inc(res_ok.sem, 1)

            def middle_tap_first(f):
                wait(dve, hT_ok, 0, 2 * f + 2)
                V.tensor_scalar(mid[:, f], hT[:, f, 1:1 + S], col_mixw[:, f, 1:2], col_mixb[:, f:f + 1],
                                ALU.mult, ALU.add).then_inc(mid_ok.sem, 1)

            def mix_before(n, f):
                wait(dve, mid_ok, n, f + 1)
                V.scalar_tensor_tensor(mixa[:, f], hT[:, f, 0:S], col_mixw[:, f, 0:1], mid[:, f],
                                       ALU.mult, ALU.add).then_inc(mix_a.sem, 1)

            def mix_after(n, f):
                wait(dve, mix_a, n, f + 1)
                V.scalar_tensor_tensor(mixT[:, f], hT[:, f, 2:S + 2], col_mixw[:, f, 2:3], mixa[:, f],
                                       ALU.mult, ALU.add).then_inc(mix.sem, 1)

            def scan_states(n):
                wait(dve, gates, n, 2)
                V.scalar_tensor_tensor(nx[:], dec[:], 1.0, xs[:], ALU.subtract, ALU.mult).then_inc(state.sem, 1)
                wait(dve, state, n, 1)
                V.tensor_tensor_scan(states[:], dec[:], nx[:], 0.0, ALU.mult, ALU.subtract).then_inc(state.sem, 1)
                wait(dve, gates, n, 4)
                wait(dve, state, n, 2)
                for f in range(NF):
                    V.tensor_tensor(selst[f * SD:(f + 1) * SD], states[:], sel[:], ALU.mult).then_inc(state.sem, 1)

            def blend(n, bank=A):
                for f in range(NF):
                    wait(dve, pe_so, n, f + 1)
                    wait(dve, u_ok, n, f + 1)
                    V.scalar_tensor_tensor(yu[:, f], bank[:, f, 0:S], col_bso[:, f:f + 1], uT[:, f],
                                           ALU.add, ALU.subtract).then_inc(yz.sem, 1)
                    wait(dve, yz, n, 3 * f + 1)
                    wait(dve, g_ok, n, f + 1)
                    V.tensor_tensor(gyu[:, f], gT[:, f], yu[:, f], ALU.mult).then_inc(yz.sem, 1)
                    wait(dve, yz, n, 3 * f + 2)
                    V.tensor_tensor(zT[:, f], gyu[:, f], uT[:, f], ALU.add).then_inc(yz.sem, 1)

            def residual(n, par):
                wait(dve, res_ok, n, NT)
                for t in RESIDUAL_ORDER:
                    if t != 1:
                        wait(dve, pe_out, n, 2 - t // 2)
                    rows = P if t < 2 else TXT
                    src = Bk[0:rows, t // 2, (t % 2) * D:(t % 2 + 1) * D]
                    V.scalar_tensor_tensor(h1[0:rows, par, t], src, nmr[0:rows, par, 0, t:t + 1], res[0:rows, t],
                                           ALU.add, ALU.add).then_inc(h1_ok.sem, 1)

            def norm2_stats(n, par):
                for k, t in enumerate(RESIDUAL_ORDER):
                    wait(dve, h1_ok, n, k + 1)
                    V.bn_stats(st2[:, t], h1[:, par, t]).then_inc(ln2.sem, 1)

            def norm2_variance(n, count):
                V.tensor_scalar(var2[:], mom2[:, :, 1], 1.0 / count, EPS, ALU.mult, ALU.add).then_inc(ln2.sem, 1)

            def norm2_bias(n):
                wait(dve, pow2, n, 1)
                V.scalar_tensor_tensor(nmr2[:], mom2[:, :, 0], -1.0, rs2[:], ALU.mult, ALU.mult).then_inc(ln2.sem, 1)

            def normalize2_first():
                wait(dve, ln2, 0, NT + 7)
                for t in range(NT):
                    V.tensor_scalar(norm2[:, t], h1[:, 0, t], rs2[:, t:t + 1], nmr2[:, t:t + 1],
                                    ALU.mult, ALU.add).then_inc(norm2_ok.sem, 1)

            def x2_low(n):
                for f in range(NF):
                    wait(dve, x2h_ok, n, f + 1)
                    V.tensor_tensor(x2l[:, f, 0:S], A[:, f, 0:S], x2h[:, f, 0:S], ALU.subtract).then_inc(x2l_ok.sem, 1)

            def hidden_low(n, q, src, high_ok, high, dst, done):
                wait(dve, high_ok, n, q + 1)
                V.scalar_tensor_tensor(dst[:, 2 * q:2 * q + 2, 0:S], src[:, :, 0:S], 0.0,
                                       high[:, 2 * q:2 * q + 2, 0:S], ALU.max, ALU.subtract).then_inc(done.sem, 1)

            def h0_low(n, q):
                hidden_low(n, q, LAYER1[q], r0h_ok, r0h, r0l, r0l_ok)

            def h1_low(n, q):
                hidden_low(n, q, LAYER2[q], r1h_ok, r1h, r1l, r1l_ok)

            def finish(n, par):
                wait_before(dve, st_out, n)
                wait(dve, pe_f3, n, 1)
                V.scalar_tensor_tensor(outb[:, 0:2].rearrange("p t w -> p (t w)"), LAYER3[:, 0, 0:2 * D],
                                       s_all[:, 1:2], h1[:, par, 0:2].rearrange("p t w -> p (t w)"),
                                       ALU.mult, ALU.add).then_inc(fin.sem, 1)
                wait(dve, pe_f3, n, 2)
                V.scalar_tensor_tensor(outb[0:TXT, 2], LAYER3[0:TXT, 1, 0:D], s_all[0:TXT, 1:2],
                                       h1[0:TXT, par, 2], ALU.mult, ALU.add).then_inc(fin.sem, 1)

            def step(b, par, mixer=True, tokens=True):
                n, t, other = b + 1, b + 2, 1 - par
                h0_low(b, 0)
                h0_low(b, 1)
                h0_low(b, 2)
                if tokens:
                    gray_green(t, par)
                    gray_blue(t, par)
                if mixer:
                    mix_before(n, 0)
                    mix_after(n, 0)
                h0_low(b, 3)
                if mixer:
                    mix_before(n, 1)
                    mix_after(n, 1)
                if tokens:
                    edges(t, par, 0, 2)
                h1_low(b, 0)
                if tokens:
                    edges(t, par, 2, 3)
                if mixer:
                    scan_states(n)
                if tokens:
                    edges(t, par, 3, 15)
                h1_low(b, 1)
                if tokens:
                    edges(t, par, 15, 16)
                if mixer:
                    blend(n)
                if tokens:
                    tokens_done(t)
                    norm1_stats(t)
                    moments(t, ln1, st1, sum1, dif1, sq1, mom1)
                    norm1_variances(t, D)
                h1_low(b, 2)
                if mixer:
                    residual(n, other)
                    norm2_stats(n, other)
                    moments(n, ln2, st2, sum2, dif2, sq2, mom2)
                    norm2_variance(n, D)
                if tokens:
                    norm1_bias(t, par)
                    residual_bias(t, par)
                if mixer:
                    norm2_bias(n)
                if tokens:
                    norm1_residual(t)
                h1_low(b, 3)
                if mixer:
                    x2_low(n)
                finish(b, par)

            dve.sem_inc(fin.sem, fin.start)
            dve.wait_ge(ld_row, 16)
            V.tensor_scalar(taps[:], taps_in, 0.5, None, ALU.mult).then_inc(prep, 1)
            dve.wait_ge(ident_set, 2)
            dve.wait_ge(prep, 1)
            for dx in range(3):
                V.tensor_scalar(tap_diag[:, 0, 0, dx], ident, taps[:, dx:dx + 1], None, ALU.mult).then_inc(tap_outer, 1)
            dve.wait_ge(tap_outer, 3)
            tap_matrices(0, 1)
            dve.wait_ge(ld_colour[1], 16)
            gray_green(0, 0)
            dve.wait_ge(cleared, 5)
            dve.wait_ge(ld_colour[2], 16)
            gray_blue(0, 0)
            dve.wait_ge(tap_diag0, 3)
            tap_matrices(0, 0)
            edge_first(0)
            gray_green(1, 1)
            edge_first(1)
            gray_blue(1, 1)
            edge_first(2)
            V.tensor_scalar(sgn[:], s_in, 0.0, None, ALU.is_ge).then_inc(prep, 1)
            edge_first(3)
            dve.wait_ge(prep, 2)
            V.tensor_scalar(sgn[:], sgn[:], 2.0, -1.0, ALU.mult, ALU.add).then_inc(prep, 1)
            edge_first(4)
            dve.wait_ge(prep, 3)
            V.tensor_scalar(w1_aff[:, 0:1], sgn[:, 1:2], 2.0 * H2_SCALE, None, ALU.mult).then_inc(prep, 1)
            V.tensor_scalar(w1_aff[:, 1:2], sgn[:, 1:2], -H2_SCALE, None, ALU.mult).then_inc(prep, 1)
            edge_first(5)
            V.tensor_tensor(s_mag[:], s_in, sgn[:], ALU.mult).then_inc(prep, 1)
            edge_first(6)
            dve.wait_ge(prep, 6)
            V.scalar_tensor_tensor(s_all[:, 0:1], s_mag[:, 0:1], 8.0 / H2_SCALE, s_mag[:, 1:2], ALU.mult, ALU.mult).then_inc(prep, 1)
            edge_first(7)
            dve.wait_ge(prep, 7)
            V.tensor_tensor(s_all[:, 1:2], s_all[:, 0:1], rows_all[:, row_at["s"][0] + 2:row_at["s"][1]], ALU.mult).then_inc(prep, 1)
            dve.wait_ge(tap_diag1, 9)
            tap_matrices(1, 0)
            tokens_done(0)
            norm1_stats(0)
            moments_first(0, ln1, st1, mom1)
            norm1_variances(0, 1)
            tap_matrices(1, 1)
            norm1_bias(0, 0)
            normalize_first(0)
            residual_bias(0, 0)
            norm1_residual(0)
            dve.wait_ge(ld_col, 16)
            middle_tap_first(0)
            mix_before(0, 0)
            middle_tap_first(1)
            mix_after(0, 0)
            mix_before(0, 1)
            mix_after(0, 1)
            dve.wait_ge(ld_k[0], 16)
            V.tensor_tensor(w0[:], k0_raw[:, 0:NF], k0_raw[:, NF:2 * NF], ALU.subtract).then_inc(w0_part, 1)
            scan_states(0)
            tokens_done(1)
            dve.wait_ge(w0_part, 1)
            V.tensor_scalar(w0[:], w0[:], sgn[:, 0:1], None, ALU.mult).then_inc(w_ready[0], 1)
            blend(0, Q[1])
            norm1_stats(1)
            residual(0, 0)
            norm2_stats(0, 0)
            moments_first(0, ln2, st2, mom2)
            norm2_variance(0, 1)
            moments_first(1, ln1, st1, mom1)
            norm1_variances(1, 1)
            norm2_bias(0)
            normalize2_first()
            x2_low(0)
            norm1_bias(1, 1)
            residual_bias(1, 1)
            dve.wait_ge(ld_k[2], 16)
            V.tensor_scalar(w2[:], k2_raw[:], 2.0, -1.0, ALU.mult, ALU.add).then_inc(w_ready[2], 1)
            norm1_residual(1)
            with dve.Fori(0, B - 3, 2) as b0:
                for par in range(2):
                    step(b0 + par, par)
            step(B - 2, 0, tokens=False)
            step(B - 1, 1, mixer=False, tokens=False)

        @block.tensor
        def _(pe):
            mm = nc.tensor.matmul

            def transposes(src, ready, n, done):
                for t in range(NT):
                    rows = P if t < 2 else TW
                    wait(pe, ready, n, t + 1)
                    for f in range(NF):
                        last = nc.tensor.transpose(A[:, f, t * P:t * P + rows], src[0:rows, t, f * P:(f + 1) * P],
                                                   ident[0:rows, 0:rows])
                        if t == NT - 1:
                            last.then_inc(done.sem, 1)

            def keep_busy(count):
                for _ in range(count):
                    mm(Q[1][:, 0, 0:P], ident, ident, start=True, stop=True)

            def conv_first(n, c, out_slots=(0, 1)):
                for out_slot in out_slots:
                    for dx in range(3):
                        for in_slot in range(2):
                            if in_slot == out_slot:
                                m = tap_diag[:, c, 1, dx]
                            else:
                                m = tap_up[:, c, dx] if in_slot else tap_down[:, c, dx]
                            last = mm(Q[n][:, c, out_slot * D:(out_slot + 1) * D], m, gray[:, n, 1 + in_slot, dx:dx + D],
                                      start=(dx == 0 and in_slot == 0), stop=(dx == 2 and in_slot == 1))
                    last.then_inc(first_conv, 1)

            def project(dst, w, f):
                for k in range(NF):
                    last = mm(dst, w[:, k, f * P:(f + 1) * P], mixT[:, k], start=(k == 0), stop=(k == NF - 1))
                return last

            def state_inputs(n):
                for k in range(NF):
                    wait(pe, mix, n, k + 1)
                    first, last = k == 0, k == NF - 1
                    sd_mm = mm(Bk[:, 0, 0:S], w_sd[:, k], mixT[:, k], start=first, stop=last)
                    if last:
                        sd_mm.then_inc(pe_sd.sem, 1)
                    for half, (lo, hi) in enumerate(SEL_TOKENS):
                        sel_mm = mm(Bk[half * SD:(half + 1) * SD, 1, 0:hi - lo], w_sel[:, k], mixT[:, k, lo:hi],
                                    start=first, stop=last)
                        if last:
                            sel_mm.then_inc(pe_sd.sem, 1)

            def u_inputs(n):
                for f in range(NF):
                    project(A[:, f, 0:S], w_i, f).then_inc(pe_u.sem, 1)

            def g_inputs(n, bank=Bk, features=range(NF)):
                if bank is Bk:
                    wait(pe, gates, n, 4)
                for f in features:
                    project(bank[:, f, 0:S], w_g, f).then_inc(pe_g.sem, 1)

            def state_output(n, bank=A):
                if bank is A:
                    wait(pe, u_ok, n, NF)
                for f in range(NF):
                    half = slice(f * SD, (f + 1) * SD)
                    wait(pe, state, n, 3 + f)
                    mm(bank[:, f, 0:S], w_so[half], selst[half], start=True, stop=True).then_inc(pe_so.sem, 1)

            def mixer_output(n):
                for k in range(NF):
                    wait(pe, yz, n, 3 * (k + 1))
                    for t in RESIDUAL_ORDER:
                        rows = P if t < 2 else TXT
                        lhs = zT[:, k, t:H:2] if t < 2 else zT[:, k, H:S]
                        last = mm(Bk[0:rows, t // 2, (t % 2) * D:(t % 2 + 1) * D], lhs, w_out[:, k],
                                  start=(k == 0 and t != 1), stop=(k == NF - 1), skip_group_check=True)
                        if k == NF - 1 and t > 0:
                            last.then_inc(pe_out.sem, 1)

            def both(dst, lhs, k, high, low, first, last):
                mm(dst, lhs, high[:, k, 0:S], start=first, stop=False)
                return mm(dst, lhs, low[:, k, 0:S], start=False, stop=last)

            def layer1(n, q):
                if q == 3:
                    wait(pe, r0l_ok, n, 1)
                if q == 2:
                    wait_before(pe, h1_ok, n + 1)
                for k in range(NF):
                    if q == 0:
                        wait(pe, x2l_ok, n, k + 1)
                    for m in range(2):
                        if q == 1 and k == 0 and not (isinstance(n, int) and n < 1):
                            wait(pe, fin, n - 1, m + 1)
                        lo = (2 * q + m) * P
                        last = both(LAYER1[q][:, m, 0:S], w0[:, k, lo:lo + P], k, x2h, x2l,
                                    k == 0, k == NF - 1)
                last.then_inc(pe_f1.sem, 1)

            def layer2(n, q):
                if q == 0:
                    wait(pe, r0l_ok, n, 2)
                if q >= 2:
                    wait(pe, r1l_ok, n, q - 1)
                for ks in (range(0, NH - 2), range(NH - 2, NH)):
                    for m in range(2):
                        lo = (2 * q + m) * P
                        for k in ks:
                            if q == 0 and m == 0:
                                pe.wait_ge(w_ready[1], k + 1)
                                if k % 2 == 0:
                                    wait(pe, r0l_ok, n, k // 2 + 1)
                            last = both(LAYER2[q][:, m, 0:S], w1[:, k, lo:lo + P], k, r0h, r0l,
                                        k == 0, k == NH - 1)
                last.then_inc(pe_f2.sem, 1)

            def layer3(n, tiles, ks):
                for t in tiles:
                    rows = P if t < 2 else TXT
                    dst = LAYER3[0:rows, t // 2, (t % 2) * D:(t % 2 + 1) * D]
                    for k in ks:
                        for part, r1 in enumerate((r1h, r1l)):
                            last = mm(dst, r1[:, k, t * P:t * P + rows], w2[:, k],
                                      start=(k == 0 and part == 0 and t != 1), stop=(k == NH - 1 and part == 1),
                                      skip_group_check=True)
                    if t > 0 and ks[-1] == NH - 1:
                        last.then_inc(pe_f3.sem, 1)

            def step(b, mixer=True):
                n = b + 1
                for q in range(NPAIR - 1):
                    layer1(b, q)
                if mixer:
                    transposes(norm, norm_ok, n, pe_t1)
                layer1(b, NPAIR - 1)
                layer2(b, 0)
                if mixer:
                    state_inputs(n)
                    u_inputs(n)
                    g_inputs(n)
                layer2(b, 1)
                if mixer:
                    state_output(n)
                layer2(b, 2)
                if mixer:
                    mixer_output(n)
                layer2(b, 3)
                early, late = range(0, NH - 2), range(NH - 2, NH)
                pe.wait_ge(w_ready[2], 1)
                wait(pe, r1l_ok, b, NPAIR - 1)
                layer3(b, range(2), early)
                if mixer:
                    transposes(norm2, norm2_ok, n, pe_t2)
                layer3(b, range(2, NT), early)
                wait(pe, r1l_ok, b, NPAIR)
                layer3(b, range(NT), late)

            pe.wait_ge(ident_set, 2)
            keep_busy(11)
            wait(pe, gray_sum, 0, 2)
            mm(Q[0][:, 1, 0:D], identw[:, 0:P], gray[:, 0, 2, 1:D + 1], start=True, stop=True)
            mm(Q[0][:, 1, D:2 * D], identw[:, 2:P + 2], gray[:, 0, 1, 1:D + 1], start=True, stop=True).then_inc(first_rows, 1)
            pe.wait_ge(tap_diag0, 6)
            pe.wait_ge(tap_mats[0], 6)
            conv_first(0, 0)
            wait(pe, gray_sum, 1, 2)
            conv_first(1, 0)
            pe.wait_ge(tap_diag1, 9)
            pe.wait_ge(tap_mats[1], 3)
            conv_first(1, 1, (0,))
            transposes(norm, norm_ok, 0, pe_t1)
            pe.wait_ge(tap_mats[1], 6)
            conv_first(1, 1, (1,))
            pe.wait_ge(ld_win, 16)
            state_inputs(0)
            u_inputs(0)
            pe.wait_ge(ld_wout, 48)
            wait(pe, edge_abs_ok, 1, 2)
            g_inputs(0, Q[0], (0,))
            state_output(0, Q[1])
            g_inputs(0, Q[0], (1,))
            mixer_output(0)
            keep_busy(15)
            transposes(norm2, norm2_ok, 0, pe_t2)
            keep_busy(2)
            pe.wait_ge(w_ready[0], 1)
            with pe.Fori(0, B - 3, 2) as b0:
                for par in range(2):
                    step(b0 + par)
            step(B - 2)
            step(B - 1, mixer=False)


_AS_THEY_ARE = ['x', 'txt', 'L0_attn_Wso', 'L0_attn_Wout', 'L0_ffn_k0', 'L0_ffn_k1', 'L0_ffn_k2']


def kernel(**inputs):
    import numpy as _np
    import concourse.bacc as _bacc
    from concourse import mybir as _mybir
    from concourse.bass_utils import run_bass_kernel_spmd as _run

    def by_feature(v):
        v = _np.asarray(v)
        return v.reshape(2, P, -1).transpose(1, 0, 2).reshape(P, -1)

    a = {name.removeprefix('L0_attn_'): _np.asarray(v) for name, v in inputs.items()}
    packs = {
        'row_pack': _np.concatenate([a['L0_tok_scharr'].ravel()] + [a[f'L0_ffn_s{i}'].reshape(1) for i in range(3)]
                                    + [a['bout']]),
        'col_pack': _np.concatenate(
            [by_feature(a[n]) for n in ('ln_g', 'ln_b', 'mix_w', 'mix_b', 'bi', 'bg', 'bso')]
            + [_np.concatenate([a['bsin'], a['bd']]).reshape(P, 1), _np.resize(a['bsel'], P).reshape(P, 1)], axis=1),
        'w_pack': _np.concatenate([a[n] for n in ('Wsin', 'Wd', 'Wsel', 'Wi', 'Wg')], axis=1),
    }
    ordered = {n: inputs[n] for n in _AS_THEY_ARE[:2]} | packs | {n: inputs[n] for n in _AS_THEY_ARE[2:]}

    nc = _bacc.Bacc("TRN2", target_bir_lowering=False, num_devices=1)
    arrays, args = {}, []
    for name, v in ordered.items():
        v = _np.ascontiguousarray(v)
        arrays[f"in_{name}_dram"] = v
        args.append(nc.dram_tensor(f"in_{name}_dram", v.shape, _mybir.dt.from_np(v.dtype), kind="ExternalInput").ap())
    shape = (inputs['x'].shape[0], inputs['x'].shape[2] + inputs['txt'].shape[1], inputs['x'].shape[3])
    args.append(nc.dram_tensor("out_0_dram", shape, _mybir.dt.float32, kind="ExternalOutput").ap())
    early_fusion_kernel(nc, *args)
    r = _run(nc, [arrays], core_ids=[0])
    return r.results[0]["out_0_dram"]
```
